# Optimizing a Trainium2 kernel written in Bass

```python
import numpy as np
import jax
import jax.numpy as jnp

def _softmax(x, axis=-1):
    return jax.nn.softmax(x, axis=axis)

def _gelu(x):
    return jax.nn.gelu(x, approximate=True)

def _silu(x):
    return jax.nn.silu(x)

def _sigmoid(x):
    return jax.nn.sigmoid(x)

def _layernorm(x, axis=-1, eps=1e-05):
    m = jnp.mean(x, axis=axis, keepdims=True)
    v = jnp.var(x, axis=axis, keepdims=True)
    return (x - m) / jnp.sqrt(v + eps)

def _scatter_add(tgt, idx, src, axis=0):
    return tgt.at[idx].add(src)

def _segment_sum(src, seg, n):
    return jax.ops.segment_sum(src, seg, n)
kernel_name = 'mk_seq_postln_d1_jaxref_r8_c0ec82'

def setup_inputs(seed: int=0):
    np.random.seed(seed)
    _w = jnp.asarray

    def _L0_attn_setup():
        import jax, jax.numpy as jnp
        import numpy as np
        D_MODEL = 128
        N_HEADS = 16
        D_HEAD = 64
        GROUP_SIZE = 2
        N_GROUPS = N_HEADS // GROUP_SIZE
        key = jax.random.key(seed)
        k1, k2, k3, k4, k5 = jax.random.split(key, 5)

        def xavier(k, shape):
            fan_in, fan_out = (shape[0], int(np.prod(shape[1:])))
            bound = float(np.sqrt(6.0 / (fan_in + fan_out)))
            return jax.random.uniform(k, shape, jnp.float32, -bound, bound)
        return {'resid': jax.random.normal(k1, (2, 256, D_MODEL), jnp.float32), 'W_Q': xavier(k2, (D_MODEL, N_HEADS, D_HEAD)), 'W_K': xavier(k3, (D_MODEL, N_GROUPS, D_HEAD)), 'W_V': xavier(k4, (D_MODEL, N_GROUPS, D_HEAD)), 'W_out': xavier(k5, (D_HEAD, N_HEADS, D_MODEL)), 'b_out': jnp.zeros((D_MODEL,), jnp.float32)}
    _L0_attn_in = _L0_attn_setup()

    def _L0_ffn_setup():
        import jax, jax.numpy as jnp
        import numpy as np
        DIM = 128
        DEPTH = 2
        HEADS = 8
        DIM_HEAD = 64
        WINDOW = 64
        INNER = HEADS * DIM_HEAD
        HID = int(DIM * 4 * 2 / 3)
        B, N = (2, 1024)
        QK_SCALE = 8.0

        def shift_token(t):
            t1, t2 = jnp.split(t, 2, axis=-1)
            t2 = jnp.pad(t2, ((0, 0), (1, 0), (0, 0)))[:, :-1]
            return jnp.concatenate([t1, t2], axis=-1)

        def l2norm(t):
            return t / jnp.clip(jnp.linalg.norm(t, axis=-1, keepdims=True), 1e-12)

        def rotate_half(x):
            x1, x2 = jnp.split(x, 2, axis=-1)
            return jnp.concatenate([-x2, x1], axis=-1)

        def rotary_xpos(q, k):
            n = q.shape[-2]
            half_idx = jnp.arange(0, DIM_HEAD, 2, dtype=jnp.float32)
            inv_freq = 1.0 / 10000.0 ** (half_idx / DIM_HEAD)
            t = jnp.arange(n, dtype=jnp.float32)
            freqs = t[:, None] * inv_freq[None, :]
            freqs = jnp.concatenate([freqs, freqs], axis=-1)
            base = (half_idx + 0.4 * DIM_HEAD) / (1.4 * DIM_HEAD)
            power = (t - n // 2) / float(WINDOW // 2)
            scale = base[None, :] ** power[:, None]
            scale = jnp.concatenate([scale, scale], axis=-1)
            cos, sin = (jnp.cos(freqs), jnp.sin(freqs))
            q = q * cos * scale + rotate_half(q) * sin * scale
            k = k * cos / scale + rotate_half(k) * sin / scale
            return (q, k)

        def local_attention(q, k, v):
            b, h, n, d = q.shape
            w = n // WINDOW
            bq = q.reshape(b, h, w, WINDOW, d) * QK_SCALE
            bk = k.reshape(b, h, w, WINDOW, d)
            bv = v.reshape(b, h, w, WINDOW, d)

            def look_around(t):
                p = jnp.pad(t, ((0, 0), (0, 0), (1, 0), (0, 0), (0, 0)))
                return jnp.concatenate([p[:, :, :w], p[:, :, 1:]], axis=3)
            bk, bv = (look_around(bk), look_around(bv))
            bt = jnp.arange(n).reshape(w, WINDOW)
            btp = jnp.pad(bt, ((1, 0), (0, 0)), constant_values=-1)
            btk = jnp.concatenate([btp[:w], btp[1:]], axis=1)
            sim = jnp.einsum('bhwid,bhwjd->bhwij', bq, bk)
            i = bt[:, :, None]
            j = btk[:, None, :]
            mask = (i < j) | (i > j + WINDOW) | (j == -1)
            sim = jnp.where(mask, -jnp.finfo(sim.dtype).max, sim)
            attn = jax.nn.softmax(sim, axis=-1)
            out = jnp.einsum('bhwij,bhwjd->bhwid', attn, bv)
            return out.reshape(b, h, n, d)

        def _layer(x, wqkv, qs, ksc, wo, lg, lb, w1, b1, w2, b2):
            b, n, _ = x.shape
            h = shift_token(x)
            qkv = h @ wqkv
            q, k, v = jnp.split(qkv, 3, axis=-1)
            to_heads = lambda t: t.reshape(b, n, HEADS, DIM_HEAD).transpose(0, 2, 1, 3)
            q, k, v = (to_heads(q), to_heads(k), to_heads(v))
            q = l2norm(q) * qs
            k = l2norm(k) * ksc
            q, k = rotary_xpos(q, k)
            o = local_attention(q, k, v)
            o = o.transpose(0, 2, 1, 3).reshape(b, n, INNER)
            x = x + o @ wo
            h = shift_token(x)
            mu = h.mean(-1, keepdims=True)
            var = h.var(-1, keepdims=True)
            h = (h - mu) / jnp.sqrt(var + 1e-05) * lg + lb
            h = h @ w1 + b1
            a, g = jnp.split(h, 2, axis=-1)
            h = a * jax.nn.gelu(g, approximate=False)
            x = x + h @ w2 + b2
            return x
        key = jax.random.key(seed)
        ks = jax.random.split(key, 6)
        return {'x': jax.random.normal(ks[0], (B, N, DIM), jnp.float32), 'wqkv': jax.random.normal(ks[1], (DEPTH, DIM, 3 * INNER), jnp.float32) * 0.02, 'q_scale': jnp.ones((DEPTH, DIM_HEAD), jnp.float32), 'k_scale': jnp.ones((DEPTH, DIM_HEAD), jnp.float32), 'wo': jax.random.normal(ks[2], (DEPTH, INNER, DIM), jnp.float32) * 0.02, 'ln_g': jnp.ones((DEPTH, DIM), jnp.float32), 'ln_b': jnp.zeros((DEPTH, DIM), jnp.float32), 'w1': jax.random.normal(ks[3], (DEPTH, DIM, 2 * HID), jnp.float32) * 0.02, 'b1': jnp.zeros((DEPTH, 2 * HID), jnp.float32), 'w2': jax.random.normal(ks[4], (DEPTH, HID, DIM), jnp.float32) * 0.02, 'b2': jnp.zeros((DEPTH, DIM), jnp.float32)}
    _L0_ffn_in = _L0_ffn_setup()
    _d = {'L0_attn_resid': _L0_attn_in['resid'], 'L0_attn_W_Q': _L0_attn_in['W_Q'], 'L0_attn_W_K': _L0_attn_in['W_K'], 'L0_attn_W_V': _L0_attn_in['W_V'], 'L0_attn_W_out': _L0_attn_in['W_out'], 'L0_attn_b_out': _L0_attn_in['b_out'], 'L0_ffn_wqkv': _L0_ffn_in['wqkv'], 'L0_ffn_q_scale': _L0_ffn_in['q_scale'], 'L0_ffn_k_scale': _L0_ffn_in['k_scale'], 'L0_ffn_wo': _L0_ffn_in['wo'], 'L0_ffn_ln_g': _L0_ffn_in['ln_g'], 'L0_ffn_ln_b': _L0_ffn_in['ln_b'], 'L0_ffn_w1': _L0_ffn_in['w1'], 'L0_ffn_b1': _L0_ffn_in['b1'], 'L0_ffn_w2': _L0_ffn_in['w2'], 'L0_ffn_b2': _L0_ffn_in['b2']}
    _x0 = _d['L0_attn_resid']
    _d['L0_attn_resid'] = jax.random.normal(jax.random.fold_in(jax.random.key(seed), 1), (8, 512, 128), dtype=_x0.dtype)
    del _x0
    return _d

def reference(L0_attn_resid, L0_attn_W_Q, L0_attn_W_K, L0_attn_W_V, L0_attn_W_out, L0_attn_b_out, L0_ffn_wqkv, L0_ffn_q_scale, L0_ffn_k_scale, L0_ffn_wo, L0_ffn_ln_g, L0_ffn_ln_b, L0_ffn_w1, L0_ffn_b1, L0_ffn_w2, L0_ffn_b2):

    def _L0_attn_ref(resid, W_Q, W_K, W_V, W_out, b_out):
        import jax, jax.numpy as jnp
        import numpy as np
        D_MODEL = 128
        N_HEADS = 16
        D_HEAD = 64
        GROUP_SIZE = 2
        N_GROUPS = N_HEADS // GROUP_SIZE
        batch, seq, _ = resid.shape
        q = jnp.einsum('bsd,dhe->bshe', resid, W_Q)
        q = q.reshape(batch, seq, N_GROUPS, GROUP_SIZE, D_HEAD)
        k = jnp.einsum('bsd,dge->bsge', resid, W_K)
        v = jnp.einsum('bsd,dge->bsge', resid, W_V)
        scores = jnp.einsum('bqgre,bkge->bgrqk', q, k) / jnp.sqrt(jnp.float32(D_HEAD))
        causal_mask = jnp.triu(jnp.ones((seq, seq), bool), k=1)
        scores = jnp.where(causal_mask, jnp.float32(-1000000.0), scores)
        probs = jax.nn.softmax(scores, axis=-1)
        z = jnp.einsum('bgrqk,bkge->bqgre', probs, v)
        z = z.reshape(batch, seq, N_HEADS, D_HEAD)
        out = jnp.einsum('bshe,ehd->bsd', z, W_out) + b_out
        return out

    def _L0_ffn_ref(x, wqkv, q_scale, k_scale, wo, ln_g, ln_b, w1, b1, w2, b2):
        import jax, jax.numpy as jnp
        import numpy as np
        DIM = 128
        DEPTH = 2
        HEADS = 8
        DIM_HEAD = 64
        WINDOW = 64
        INNER = HEADS * DIM_HEAD
        HID = int(DIM * 4 * 2 / 3)
        B, N = (2, 1024)
        QK_SCALE = 8.0

        def shift_token(t):
            t1, t2 = jnp.split(t, 2, axis=-1)
            t2 = jnp.pad(t2, ((0, 0), (1, 0), (0, 0)))[:, :-1]
            return jnp.concatenate([t1, t2], axis=-1)

        def l2norm(t):
            return t / jnp.clip(jnp.linalg.norm(t, axis=-1, keepdims=True), 1e-12)

        def rotate_half(x):
            x1, x2 = jnp.split(x, 2, axis=-1)
            return jnp.concatenate([-x2, x1], axis=-1)

        def rotary_xpos(q, k):
            n = q.shape[-2]
            half_idx = jnp.arange(0, DIM_HEAD, 2, dtype=jnp.float32)
            inv_freq = 1.0 / 10000.0 ** (half_idx / DIM_HEAD)
            t = jnp.arange(n, dtype=jnp.float32)
            freqs = t[:, None] * inv_freq[None, :]
            freqs = jnp.concatenate([freqs, freqs], axis=-1)
            base = (half_idx + 0.4 * DIM_HEAD) / (1.4 * DIM_HEAD)
            power = (t - n // 2) / float(WINDOW // 2)
            scale = base[None, :] ** power[:, None]
            scale = jnp.concatenate([scale, scale], axis=-1)
            cos, sin = (jnp.cos(freqs), jnp.sin(freqs))
            q = q * cos * scale + rotate_half(q) * sin * scale
            k = k * cos / scale + rotate_half(k) * sin / scale
            return (q, k)

        def local_attention(q, k, v):
            b, h, n, d = q.shape
            w = n // WINDOW
            bq = q.reshape(b, h, w, WINDOW, d) * QK_SCALE
            bk = k.reshape(b, h, w, WINDOW, d)
            bv = v.reshape(b, h, w, WINDOW, d)

            def look_around(t):
                p = jnp.pad(t, ((0, 0), (0, 0), (1, 0), (0, 0), (0, 0)))
                return jnp.concatenate([p[:, :, :w], p[:, :, 1:]], axis=3)
            bk, bv = (look_around(bk), look_around(bv))
            bt = jnp.arange(n).reshape(w, WINDOW)
            btp = jnp.pad(bt, ((1, 0), (0, 0)), constant_values=-1)
            btk = jnp.concatenate([btp[:w], btp[1:]], axis=1)
            sim = jnp.einsum('bhwid,bhwjd->bhwij', bq, bk)
            i = bt[:, :, None]
            j = btk[:, None, :]
            mask = (i < j) | (i > j + WINDOW) | (j == -1)
            sim = jnp.where(mask, -jnp.finfo(sim.dtype).max, sim)
            attn = jax.nn.softmax(sim, axis=-1)
            out = jnp.einsum('bhwij,bhwjd->bhwid', attn, bv)
            return out.reshape(b, h, n, d)

        def _layer(x, wqkv, qs, ksc, wo, lg, lb, w1, b1, w2, b2):
            b, n, _ = x.shape
            h = shift_token(x)
            qkv = h @ wqkv
            q, k, v = jnp.split(qkv, 3, axis=-1)
            to_heads = lambda t: t.reshape(b, n, HEADS, DIM_HEAD).transpose(0, 2, 1, 3)
            q, k, v = (to_heads(q), to_heads(k), to_heads(v))
            q = l2norm(q) * qs
            k = l2norm(k) * ksc
            q, k = rotary_xpos(q, k)
            o = local_attention(q, k, v)
            o = o.transpose(0, 2, 1, 3).reshape(b, n, INNER)
            x = x + o @ wo
            h = shift_token(x)
            mu = h.mean(-1, keepdims=True)
            var = h.var(-1, keepdims=True)
            h = (h - mu) / jnp.sqrt(var + 1e-05) * lg + lb
            h = h @ w1 + b1
            a, g = jnp.split(h, 2, axis=-1)
            h = a * jax.nn.gelu(g, approximate=False)
            x = x + h @ w2 + b2
            return x
        for l in range(DEPTH):
            x = _layer(x, wqkv[l], q_scale[l], k_scale[l], wo[l], ln_g[l], ln_b[l], w1[l], b1[l], w2[l], b2[l])
        return x
    x = L0_attn_resid
    x = _layernorm(x + _L0_attn_ref(x, L0_attn_W_Q, L0_attn_W_K, L0_attn_W_V, L0_attn_W_out, L0_attn_b_out), axis=-1)
    x = _layernorm(x + _L0_ffn_ref(x, L0_ffn_wqkv, L0_ffn_q_scale, L0_ffn_k_scale, L0_ffn_wo, L0_ffn_ln_g, L0_ffn_ln_b, L0_ffn_w1, L0_ffn_b1, L0_ffn_w2, L0_ffn_b2), axis=-1)
    return x

_drawn_inputs = setup_inputs


def setup_inputs(seed=0):
    import zlib

    import numpy as np

    out = dict(_drawn_inputs(seed))
    spreads = {'L0_attn_b_out': (0.0, 0.1),
     'L0_ffn_q_scale': (1.0, 0.6),
     'L0_ffn_k_scale': (1.0, 0.6),
     'L0_ffn_ln_g': (1.0, 0.6),
     'L0_ffn_ln_b': (0.0, 0.8),
     'L0_ffn_b1': (0.0, 0.8),
     'L0_ffn_b2': (0.0, 0.453)}
    factors = {'L0_ffn_wqkv': 3.451, 'L0_ffn_wo': 3.454, 'L0_ffn_w1': 6.204, 'L0_ffn_w2': 6.119}
    for name, (base, spread) in spreads.items():
        noise = np.random.default_rng([zlib.crc32(name.encode()), seed]).standard_normal(out[name].shape)
        drawn = base * np.exp(spread * noise) if base else spread * noise
        out[name] = jnp.asarray(drawn.astype(out[name].dtype))
    for name, factor in factors.items():
        out[name] = (out[name] * factor).astype(out[name].dtype)
    return out
```

```python
from contextlib import ExitStack

import numpy as np

import concourse.bass as bass
from concourse import mybir
from concourse.alu_op_type import AluOpType as ALU

ACT = mybir.ActivationFunctionType
AX = mybir.AxisListType
F32 = mybir.dt.float32
BF16 = mybir.dt.bfloat16

P = 128
B, S, D = 8, 512, 128
NT = S // P
E = 64
HA, GA = 16, 8
CA = HA // 2
UNITS = CA * NT
LAYERS, HB = 2, 8
CB = HB // 2
WIN = 64
INNER = HB * E
HID = 341
CH = 3
MCH = [128, 128, HID - 256]
EPS = 1e-5
B2ROW = 96
MASKED = -1e30


def merged():
    a = [("a_turn_x", 0)] + [("a_project", r) for r in range(4)]
    for n in range(UNITS):
        a += [("a_scores", n)]
        if n:
            a += [("a_turn", n - 1), ("a_value", n - 1)]
    a += [("a_turn", UNITS - 1), ("a_value", UNITS - 1), ("a_out", 0)]
    b = []
    for l in range(LAYERS):
        b += [("b_shift", (l, 0)), ("b_qkv", (l, 0)), ("b_turn_qk", (l, 0))]
        for t in range(NT):
            if t + 1 < NT:
                b += [("b_qkv", (l, t + 1))]
            b += [("b_scores", (l, t)), ("b_turn_p", (l, t)), ("b_value", (l, t)), ("b_wo", (l, t))]
            if t + 1 < NT:
                b += [("b_turn_qk", (l, t + 1))]
        b += [("b_norm", (l, 0)), ("b_turn_f", (l, 0)), ("b_ffn", (l, 0)), ("b_w2", (l, 0))]
    b += [("b_final", (LAYERS - 1, 0))]
    order, done = [], 0
    for n, step in enumerate(a):
        if step[0] == "a_out":
            break
        order.append(step)
        upto = (n + 1) * len(b) // (len(a) - 1)
        order += b[done:upto]
        done = upto
    return order + b[done:] + [a[-1]]


ORDER = merged()
CHAIN_A, CHAIN_B = 2, 4


def program(nc, t_in, out):
    ctx = ExitStack()
    with ctx:
        def sb(name, shape, dt=F32):
            return ctx.enter_context(nc.sbuf_tensor(name, shape, dt))

        def ps(name, shape):
            return ctx.enter_context(nc.psum_tensor(name, shape, F32))

        def sem(name):
            return ctx.enter_context(nc.semaphore(name))

        ident, ident_b = sb("ident", [P, P]), sb("ident_b", [P, P], BF16)
        causal = sb("causal", [P, P], BF16)
        band = sb("band", [P, 2, P], BF16)
        shift_m, last_m = sb("shift_m", [P, P]), sb("last_m", [P, P])
        rope = sb("rope", [P, 2, NT, 2, E])
        scale_bc = sb("scale_bc", [P, LAYERS, 2, E])
        table = sb("table", [P, LAYERS, 2, NT, 2, E])
        wq, wk, wv = sb("wq", [P, CA, P]), sb("wk", [P, GA // 2, P]), sb("wv", [P, GA * E])
        wout, bout = sb("wout", [P, CA, D]), sb("bout", [P, D])
        wqkv, wo = sb("wqkv", [P, LAYERS, 3 * INNER]), sb("wo", [P, LAYERS, CB, D])
        w1, w2 = sb("w1", [P, LAYERS, 2 * HID]), sb("w2", [P, LAYERS, CH, D])
        b1 = sb("b1", [P, LAYERS, 2, CH])
        ln_gb = sb("ln_gb", [P, LAYERS, 2])
        x_in, x_res, x_t = sb("x_in", [P, NT, D]), sb("x_res", [P, NT, D]), sb("x_t", [P, S])
        q_t, k_t, v = sb("q_t", [P, CA, S]), sb("k_t", [P, GA // 2, S]), sb("v", [P, NT, GA * E])
        negmax, rowsum, rowinv = sb("negmax", [P, 2, 2]), sb("rowsum", [P, 2, 2]), sb("rowinv", [P, 2, 2])
        prob, prob_t = sb("prob", [P, 2, 2, S]), sb("prob_t", [P, 2, 2, S])
        z_t, y = sb("z_t", [P, CA, S]), sb("y", [P, NT, D])
        st_a, mv_a, ve_a, rs_a = sb("st_a", [P, NT, 6]), sb("mv_a", [P, NT, 2]), sb("ve_a", [P, NT]), sb("rs_a", [P, NT])
        x1 = sb("x1", [P, NT, D])
        h_t = sb("h_t", [P, S])
        qk, sq = sb("qk", [P, 2, HB, E]), sb("sq", [P, 2, HB, E])
        r1, r2, rot = sb("r1", [P, 2, HB, E]), sb("r2", [P, 2, HB, E]), sb("rot", [P, 2, HB, E])
        ssq, ssq_floor, rnorm = sb("ssq", [P, 2 * HB]), sb("ssq_floor", [P, 2 * HB]), sb("rnorm", [P, 2 * HB])
        minus_half = sb("minus_half", [P, 2 * HB])
        qb_t, kb_t = sb("qb_t", [P, CB, P]), sb("kb_t", [P, CB, WIN + S])
        vb, vb_mid = sb("vb", [P, NT, INNER]), sb("vb_mid", [P, NT, INNER])
        b_negmax, b_rowsum, b_rowinv = sb("b_negmax", [P, HB]), sb("b_rowsum", [P, HB]), sb("b_rowinv", [P, HB])
        b_prob, b_prob_t = sb("b_prob", [P, 2, CB, P]), sb("b_prob_t", [P, 2, CB, P])
        o_t = sb("o_t", [P, CB, P])
        x2, x3 = sb("x2", [P, NT, D]), sb("x3", [P, NT, D])
        st_b, mv_b, ve_b, rs_b = sb("st_b", [P, NT, 12]), sb("mv_b", [P, NT, 2]), sb("ve_b", [P, NT]), sb("rs_b", [P, NT])
        x_hat, f_t = sb("x_hat", [P, NT, D]), sb("f_t", [P, S])
        gelu, u_t = sb("gelu", [P, 2, S]), sb("u_t", [P, CH, S])
        y_out = sb("y_out", [P, NT, D])

        a_scores, a_turned, a_z = ps("a_scores", [P, 2, 512]), ps("a_turned", [P, 2, 512]), ps("a_z", [P, 512])
        b_pair, b_misc = ps("b_pair", [P, 2, 512]), ps("b_misc", [P, 512])

        early_in, late_in, tables_in = sem("early_in"), sem("late_in"), sem("tables_in")
        consts_ready = sem("consts_ready")
        x_loaded, x_turned, x_t_ready, x_res_ready = sem("x_loaded"), sem("x_turned"), sem("x_t_ready"), sem("x_res_ready")
        projected, proj_act, proj_dve = sem("projected"), sem("proj_act"), sem("proj_dve")
        scored, negmax_ready, exp_done = sem("scored"), sem("negmax_ready"), sem("exp_done")
        rowinv_ready, prob_ready, turned = sem("rowinv_ready"), sem("prob_ready"), sem("turned")
        prob_t_act, prob_t_dve, valued, z_ready = sem("prob_t_act"), sem("prob_t_dve"), sem("valued"), sem("z_ready")
        out_done, chain_a, x1_ready = sem("out_done"), sem("chain_a"), sem("x1_ready")
        var_a_ready, eps_a_ready, rs_a_ready = sem("var_a_ready"), sem("eps_a_ready"), sem("rs_a_ready")
        half_ready = sem("half_ready")
        B_SEMS = {}

        def bsem(name, engine):
            s = sem(name)
            B_SEMS.setdefault(engine, []).append(s)
            return s

        h_done, h_ready = bsem("h_done", "pe"), bsem("h_ready", "act")
        qkv_done, qk_ready, vb_ready = bsem("qkv_done", "pe"), bsem("qk_ready", "act"), bsem("vb_ready", "act")
        sq_ready, r1_ready, r2_ready = bsem("sq_ready", "act"), bsem("r1_ready", "dve"), bsem("r2_ready", "dve")
        ssq_ready, floor_ready, rnorm_ready = bsem("ssq_ready", "dve"), bsem("floor_ready", "pool"), bsem("rnorm_ready", "pool")
        var_b_ready, eps_b_ready, rs_b_ready = bsem("var_b_ready", "dve"), bsem("eps_b_ready", "pool"), bsem("rs_b_ready", "pool")
        rsum_ready, rot_ready, qk_turned = bsem("rsum_ready", "pool"), bsem("rot_ready", "pool"), bsem("qk_turned", "pe")
        qb_ready, kb_ready = bsem("qb_ready", "act"), bsem("kb_ready", "dve")
        b_scored, b_negmax_ready, b_exp_done = bsem("b_scored", "pe"), bsem("b_negmax_ready", "dve"), bsem("b_exp_done", "act")
        b_rowinv_ready, b_prob_ready, b_turned = bsem("b_rowinv_ready", "dve"), bsem("b_prob_ready", "pool"), bsem("b_turned", "pe")
        b_pt_act, b_pt_dve = bsem("b_pt_act", "act"), bsem("b_pt_dve", "dve")
        b_valued, o_ready, wo_done, x2_ready = bsem("b_valued", "pe"), bsem("o_ready", "act"), bsem("wo_done", "pe"), bsem("x2_ready", "dve")
        shifted, chain_b, x_hat_ready = bsem("shifted", "pe"), bsem("chain_b", "dve"), bsem("x_hat_ready", "dve")
        f_turned, f_ready, w1_done = bsem("f_turned", "pe"), bsem("f_ready", "act"), bsem("w1_done", "pe")
        gelu_done, u_ready, w2_done, x3_ready = bsem("gelu_done", "act"), bsem("u_ready", "dve"), bsem("w2_done", "pe"), bsem("x3_ready", "dve")
        y_out_ready = bsem("y_out_ready", "dve")
        y_stored = sem("y_stored")
        v_hi = [sem(f"v_hi{t}") for t in range(NT)]
        v_lo = [sem(f"v_lo{t}") for t in range(NT)]

        def head_bank(i):
            return (a_scores if i % 4 < 2 else a_turned)[:, i % 2, :]

        def units_pair(n):
            return n // NT, n % NT, P * (n % NT + 1)

        def walk(a_index, b_index, steps):
            for name, arg in ORDER:
                if name in steps:
                    if name[0] == "a" and a_index is not None:
                        steps[name](a_index, arg)
                    if name[0] == "b" and b_index is not None:
                        steps[name](b_index, *arg)

        def all_sequences(eng, steps):
            walk(0, None, steps)
            with eng.Fori(1, B) as b:
                walk(b, b - 1, steps)
            walk(None, B - 1, steps)

        def need(eng, s, value):
            if not (type(value) is int and value <= 0):
                eng.wait_ge(s, value)

        waited_dve, waited_pool = sem("waited_dve"), sem("waited_pool")

        def wait_apart(eng, passed, s, value):
            eng.wait_ge(s, value)
            eng.sem_inc(passed, 1)

        block = ctx.enter_context(nc.Block())

        @block.sync
        def _(sp):
            for dst, src in ((ident, "ident"), (causal, "causal"), (ident_b, "ident_b"), (wq, "wq"), (wk, "wk"),
                             (wv, "wv"), (wout, "wout")):
                sp.dma_start(dst[:], t_in[src]).then_inc(early_in, 16)
            sp.dma_start(bout[:], t_in["bout"].partition_broadcast(P)).then_inc(early_in, 16)
            sp.sem_inc(y_stored, 16)

            def load(b, _):
                need(sp, x_turned, b)
                need(sp, x_res_ready, b)
                src = t_in["x"][b] if type(b) is int else t_in["x"][bass.ds(b, 1)].rearrange("o s d -> (o s) d")
                sp.dma_start(x_in[:], src.rearrange("(t p) d -> p t d", p=P)).then_inc(x_loaded, 16)

            load(0, 0)
            sp.dma_start(rope[:], t_in["rope"]).then_inc(tables_in, 16)
            sp.dma_start(scale_bc[:], t_in["scales"].partition_broadcast(P)).then_inc(tables_in, 16)
            for dst, src in ((band, "band"), (shift_m, "shift_m"), (last_m, "last_m"), (wqkv, "wqkv"), (wo, "wo"),
                             (w1, "w1"), (w2, "w2"), (b1, "b1"), (ln_gb, "ln_gb")):
                sp.dma_start(dst[:], t_in[src]).then_inc(late_in, 16)

            def v_shift(b, l, t):
                sp.wait_ge(vb_ready, 8 * b + 4 * l + t + 2)
                sp.dma_start(vb_mid[WIN:P, t, :], vb[0:WIN, t, :]).then_inc(v_hi[t], 16)
                if t + 1 < NT:
                    sp.dma_start(vb_mid[0:WIN, t + 1, :], vb[WIN:P, t, :]).then_inc(v_lo[t + 1], 16)

            def store(b, l, _):
                sp.wait_ge(y_out_ready, b + 2)
                if type(b) is int:
                    dst = out[b]
                else:
                    dst = out[bass.ds(b, 1)].rearrange("o s d -> (o s) d")
                sp.dma_start(dst.rearrange("(t p) d -> p t d", p=P), y_out[:]).then_inc(y_stored, 16)

            steps = {"a_turn_x": load, "b_qkv": v_shift, "b_final": store}
            with sp.Fori(1, B) as b:
                walk(b, b - 1, steps)
            walk(None, B - 1, steps)
            sp.wait_ge(y_stored, 16 * (B + 1))

        @block.tensor
        def _(pe):
            for s in B_SEMS["pe"]:
                pe.sem_inc(s, 1)
            pe.wait_ge(early_in, 16 * 8)
            mm = nc.tensor.matmul

            def turn_x(b, _):
                pe.wait_ge(x_loaded, 16 * (b + 1))
                need(pe, prob_t_dve, UNITS * b)
                for t in range(NT):
                    last = nc.tensor.transpose(a_turned[:, 1, t * P:(t + 1) * P], x_in[:, t, :], ident[:])
                last.then_inc(x_turned, 1)

            def project(b, r):
                for i in range(4 * r, 4 * r + 4):
                    if i == 0:
                        pe.wait_ge(x_t_ready, b + 1)
                        need(pe, exp_done, UNITS * b)
                        need(pe, x1_ready, b)
                    if i >= 4:
                        pe.wait_ge(proj_dve if i % 2 else proj_act, 8 * b + i // 2 - 1)
                    if i < 8:
                        last = mm(head_bank(i), wq[:, i, :], x_t[:], start=True, stop=True)
                    elif i < 12:
                        last = mm(head_bank(i), wk[:, i - 8, :], x_t[:], start=True, stop=True)
                    else:
                        last = mm(head_bank(i), x_t[:, (i - 12) * P:(i - 11) * P], wv[:], start=True, stop=True)
                    last.then_inc(projected, 1)

            def scores(b, n):
                c, i, w = units_pair(n)
                if n == 0:
                    pe.wait_ge(proj_act, 8 * b + 8)
                    pe.wait_ge(proj_dve, 8 * b + 8)
                else:
                    pe.wait_ge(exp_done, UNITS * b + n)
                for h in range(2):
                    half = slice(E * h, E * h + E)
                    mm(a_scores[:, h, 0:w], q_t[half, c, i * P:(i + 1) * P], k_t[half, c // 2, 0:w],
                       start=True, stop=False)
                for h in range(2):
                    last = mm(a_scores[:, h, w - P:w], ident_b[:], causal[:], start=False, stop=True)
                last.then_inc(scored, 1)

            def turn(b, n):
                _, i, _ = units_pair(n)
                pe.wait_ge(prob_ready, UNITS * b + n + 1)
                if n:
                    pe.wait_ge(prob_t_act, UNITS * b + n)
                    pe.wait_ge(prob_t_dve, UNITS * b + n)
                for h in range(2):
                    for j in range(i + 1):
                        last = nc.tensor.transpose(a_turned[:, h, j * P:(j + 1) * P],
                                                   prob[:, n % 2, h, j * P:(j + 1) * P], ident[:])
                last.then_inc(turned, 1)

            def value(b, n):
                c, i, _ = units_pair(n)
                pe.wait_ge(prob_t_act, UNITS * b + n + 1)
                pe.wait_ge(prob_t_dve, UNITS * b + n + 1)
                if i == 0:
                    need(pe, z_ready, CA * b + c)
                for j in range(i + 1):
                    for h in range(2):
                        g = 2 * (c // 2) + h
                        last = mm(a_z[E * h:E * h + E, i * P:(i + 1) * P], v[:, j, g * E:(g + 1) * E],
                                  prob_t[:, n % 2, h, j * P:(j + 1) * P], start=(j == 0), stop=(j == i))
                last.then_inc(valued, 1)

            def out_a(b, _):
                pe.wait_ge(z_ready, CA * b + CA)
                for t in range(NT):
                    for c in range(CA):
                        last = mm(a_turned[:, 0, t * P:(t + 1) * P], z_t[:, c, t * P:(t + 1) * P], wout[:, c, :],
                                  start=(c == 0), stop=(c == CA - 1))
                last.then_inc(out_done, 1)

            def shift(b, l, _):
                src = x1 if l == 0 else x3
                if l == 0:
                    pe.wait_ge(x1_ready, b + 1)
                pe.wait_ge(x3_ready, 2 * b + l + 1)
                for t in range(NT):
                    cols = slice(t * P, (t + 1) * P)
                    mm(b_misc[0:E, cols], src[:, t, 0:E], ident[:], start=True, stop=True)
                    last = mm(b_misc[E:P, cols], src[:, t, E:P], shift_m[:], start=True, stop=(t == 0))
                    if t:
                        last = mm(b_misc[E:P, cols], src[:, t - 1, E:P], last_m[:], start=False, stop=True)
                last.then_inc(h_done, 1)

            def qkv(b, l, t):
                T = 8 * b + 4 * l + t
                if t == 0:
                    pe.wait_ge(h_ready, 2 * b + l + 2)
                    pe.wait_ge(u_ready, CH * (2 * b + l) + 1)
                else:
                    pe.wait_ge(qb_ready, T + 1)
                    pe.wait_ge(kb_ready, T + 1)
                    pe.wait_ge(o_ready, T)
                lhs = h_t[:, t * P:(t + 1) * P]
                mm(b_pair[:, 0, :], lhs, wqkv[:, l, 0:INNER], start=True, stop=True)
                mm(b_pair[:, 1, :], lhs, wqkv[:, l, INNER:2 * INNER], start=True, stop=True)
                mm(b_misc[:], lhs, wqkv[:, l, 2 * INNER:], start=True, stop=True).then_inc(qkv_done, 1)

            def turn_qk(b, l, t):
                T = 8 * b + 4 * l + t
                pe.wait_ge(rot_ready, T + 2)
                pe.wait_ge(x2_ready, T + 1)
                for s in range(2):
                    for c in range(CB):
                        last = nc.tensor.transpose(b_pair[:, s, c * P:(c + 1) * P],
                                                   rot[:, s, 2 * c:2 * c + 2, :].rearrange("p h e -> p (h e)"), ident[:])
                last.then_inc(qk_turned, 1)

            def b_score(b, l, t):
                T = 8 * b + 4 * l + t
                pe.wait_ge(qb_ready, T + 2)
                pe.wait_ge(kb_ready, T + 2)
                if t + 1 < NT:
                    pe.wait_ge(qk_ready, T + 3)
                for s in range(2):
                    mm(b_pair[:, s, :], ident_b[:],
                       band[:, min(t, 1), :].unsqueeze(1).broadcast_to([P, CB, P]), start=True, stop=True)
                for c in range(CB):
                    for w in range(2):
                        for s in range(2):
                            half = slice(E * s, E * s + E)
                            k0 = t * P + WIN * w
                            last = mm(b_pair[WIN * w:WIN * w + WIN, s, c * P:(c + 1) * P],
                                      qb_t[half, c, WIN * w:WIN * w + WIN], kb_t[half, c, k0:k0 + P],
                                      start=False, stop=True, skip_group_check=True)
                last.then_inc(b_scored, 1)

            def b_turn(b, l, t):
                pe.wait_ge(b_prob_ready, 8 * b + 4 * l + t + 2)
                for s in range(2):
                    for c in range(CB):
                        last = nc.tensor.transpose(b_pair[:, s, c * P:(c + 1) * P], b_prob[:, s, c, :], ident[:])
                last.then_inc(b_turned, 1)

            def b_value(b, l, t):
                T = 8 * b + 4 * l + t
                pe.wait_ge(b_pt_act, T + 2)
                pe.wait_ge(b_pt_dve, T + 2)
                pe.wait_ge(v_hi[t], 16 * (2 * b + l) + 16)
                if t:
                    pe.wait_ge(v_lo[t], 16 * (2 * b + l) + 16)
                if t + 1 < NT:
                    pe.wait_ge(vb_ready, T + 3)
                for c in range(CB):
                    for w in range(2):
                        for s in range(2):
                            h = 2 * c + s
                            src = vb if w else vb_mid
                            last = mm(b_misc[E * s:E * s + E, c * P + WIN * w:c * P + WIN * w + WIN],
                                      src[:, t, h * E:(h + 1) * E], b_prob_t[:, s, c, WIN * w:WIN * w + WIN],
                                      start=True, stop=True)
                last.then_inc(b_valued, 1)

            def b_wo(b, l, t):
                pe.wait_ge(o_ready, 8 * b + 4 * l + t + 2)
                for c in range(CB):
                    last = mm(b_pair[:, 0, 0:D], o_t[:, c, :], wo[:, l, c, :], start=(c == 0), stop=(c == CB - 1))
                last.then_inc(wo_done, 1)

            def norm(b, l, _):
                pe.wait_ge(x2_ready, 8 * b + 4 * l + 5)
                for t in range(NT):
                    cols = slice(t * E, (t + 1) * E)
                    last = mm(b_misc[:, cols], shift_m[:], x2[:, t, E:P], start=True, stop=(t == 0))
                    if t:
                        last = mm(b_misc[:, cols], last_m[:], x2[:, t - 1, E:P], start=False, stop=True)
                last.then_inc(shifted, 1)

            def turn_f(b, l, _):
                pe.wait_ge(x_hat_ready, 2 * b + l + 2)
                for t in range(NT):
                    last = nc.tensor.transpose(b_misc[:, t * P:(t + 1) * P], x_hat[:, t, :], ident[:])
                last.then_inc(f_turned, 1)

            def ffn(b, l, _):
                L = 2 * b + l
                pe.wait_ge(f_ready, L + 2)
                for m in range(2 * CH):
                    ch, part = m // 2, 1 - m % 2
                    if m == 3:
                        pe.wait_ge(gelu_done, CH * L + 2)
                    if m == 4:
                        pe.wait_ge(u_ready, CH * L + 2)
                    if m == 5:
                        pe.wait_ge(gelu_done, CH * L + 3)
                    bank = b_misc[:] if m % 3 == 2 else b_pair[:, m % 3, :]
                    o = part * HID + ch * P
                    mm(bank[0:MCH[ch], :], w1[:, l, o:o + MCH[ch]], f_t[:], start=True, stop=True).then_inc(w1_done, 1)

            def w2_mul(b, l, _):
                L = 2 * b + l
                pe.wait_ge(u_ready, CH * L + CH + 1)
                for t in range(NT):
                    for ch in range(CH):
                        last = mm(b_misc[:, t * P:(t + 1) * P], u_t[:, ch, t * P:(t + 1) * P], w2[:, l, ch, :],
                                  start=(ch == 0), stop=(ch == CH - 1))
                last.then_inc(w2_done, 1)

            steps = {"a_turn_x": turn_x, "a_project": project, "a_scores": scores, "a_turn": turn, "a_value": value,
                     "a_out": out_a, "b_shift": shift, "b_qkv": qkv, "b_turn_qk": turn_qk, "b_scores": b_score,
                     "b_turn_p": b_turn, "b_value": b_value, "b_wo": b_wo, "b_norm": norm, "b_turn_f": turn_f,
                     "b_ffn": ffn, "b_w2": w2_mul}
            walk(0, None, steps)
            pe.wait_ge(late_in, 16 * 9)
            pe.wait_ge(consts_ready, 2)
            with pe.Fori(1, B) as b:
                walk(b, b - 1, steps)
            walk(None, B - 1, steps)

        @block.scalar
        def _(act):
            for s in B_SEMS["act"]:
                act.sem_inc(s, 1)
            af = nc.scalar.activation

            def turn_x(b, _):
                act.wait_ge(x_turned, b + 1)
                nc.scalar.copy(x_t[:], a_turned[:, 1, :]).then_inc(x_t_ready, 1)

            def project(b, r):
                for i in range(4 * r, 4 * r + 4, 2):
                    act.wait_ge(projected, 16 * b + i + 1)
                    if i < 8:
                        last = nc.scalar.mul(q_t[:, i, :], head_bank(i), E ** -0.5)
                    elif i < 12:
                        last = nc.scalar.copy(k_t[:, i - 8, :], head_bank(i))
                    else:
                        last = nc.scalar.copy(v[:, i - 12, :], head_bank(i))
                    last.then_inc(proj_act, 1)

            def exponentials(b, n):
                _, _, w = units_pair(n)
                N = UNITS * b + n
                act.wait_ge(negmax_ready, N + 1)
                need(act, turned, N - 1)
                for h in range(2):
                    last = af(prob[:, n % 2, h, 0:w], a_scores[:, h, 0:w], ACT.Exp, bias=negmax[:, n % 2, h:h + 1],
                              accum_out=rowsum[:, n % 2, h:h + 1])
                last.then_inc(exp_done, 1)

            def turn(b, n):
                _, _, w = units_pair(n)
                N = UNITS * b + n
                act.wait_ge(turned, N + 1)
                need(act, valued, N - 1)
                nc.scalar.copy(prob_t[:, n % 2, 0, 0:w], a_turned[:, 0, 0:w]).then_inc(prob_t_act, 1)

            def value(b, n):
                c, i, _ = units_pair(n)
                if i == NT - 1:
                    act.wait_ge(valued, UNITS * b + n + 1)
                    need(act, out_done, b)
                    nc.scalar.copy(z_t[:, c, :], a_z[:]).then_inc(z_ready, 1)

            def shift(b, l, _):
                act.wait_ge(h_done, 2 * b + l + 2)
                nc.scalar.copy(h_t[:], b_misc[:]).then_inc(h_ready, 1)

            def qkv(b, l, t):
                T = 8 * b + 4 * l + t
                act.wait_ge(qkv_done, T + 2)
                act.wait_ge(r2_ready, T + 1)
                act.wait_ge(sq_ready, T + 1)
                nc.scalar.copy(qk[:].rearrange("p s h e -> p s (h e)"), b_pair[:]).then_inc(qk_ready, 1)
                nc.scalar.copy(vb[:, t, :], b_misc[:]).then_inc(vb_ready, 1)
                act.wait_ge(qk_ready, T + 2)
                act.wait_ge(ssq_ready, T + 1)
                af(sq[:], qk[:], ACT.Square).then_inc(sq_ready, 1)

            def turn_qk(b, l, t):
                act.wait_ge(qk_turned, 8 * b + 4 * l + t + 2)
                nc.scalar.copy(qb_t[:].rearrange("p c n -> p (c n)"), b_pair[:, 0, :]).then_inc(qb_ready, 1)

            def b_exp(b, l, t):
                act.wait_ge(b_negmax_ready, 8 * b + 4 * l + t + 2)
                for s in range(2):
                    for c in range(CB):
                        k = s * CB + c
                        last = af(b_prob[:, s, c, :], b_pair[:, s, c * P:(c + 1) * P], ACT.Exp,
                                  bias=b_negmax[:, k:k + 1], accum_out=b_rowsum[:, k:k + 1])
                last.then_inc(b_exp_done, 1)

            def b_turn(b, l, t):
                act.wait_ge(b_turned, 8 * b + 4 * l + t + 2)
                nc.scalar.copy(b_prob_t[:, 0, :, :].rearrange("p c n -> p (c n)"), b_pair[:, 0, :]).then_inc(b_pt_act, 1)

            def b_value(b, l, t):
                act.wait_ge(b_valued, 8 * b + 4 * l + t + 2)
                nc.scalar.copy(o_t[:].rearrange("p c n -> p (c n)"), b_misc[:]).then_inc(o_ready, 1)

            def turn_f(b, l, _):
                act.wait_ge(f_turned, 2 * b + l + 2)
                af(f_t[:], b_misc[:], ACT.Identity, scale=ln_gb[:, l, 0:1], bias=ln_gb[:, l, 1:2]).then_inc(f_ready, 1)

            def ffn(b, l, _):
                L = 2 * b + l
                for ch in range(CH):
                    m, k = 2 * ch, MCH[ch]
                    bank = b_misc[:] if m % 3 == 2 else b_pair[:, m % 3, :]
                    act.wait_ge(w1_done, 6 * L + m + 2)
                    act.wait_ge(u_ready, CH * L + ch if ch else CH * L + 1)
                    af(gelu[0:k, ch % 2, :], bank[0:k, :], ACT.Gelu, bias=b1[0:k, l, 1, ch:ch + 1]).then_inc(gelu_done, 1)

            steps = {"a_turn_x": turn_x, "a_project": project, "a_scores": exponentials, "a_turn": turn,
                     "a_value": value, "b_shift": shift, "b_qkv": qkv, "b_turn_qk": turn_qk, "b_scores": b_exp,
                     "b_turn_p": b_turn, "b_value": b_value, "b_turn_f": turn_f, "b_ffn": ffn}
            walk(0, None, steps)
            act.wait_ge(late_in, 16 * 9)
            with act.Fori(1, B) as b:
                walk(b, b - 1, steps)
            walk(None, B - 1, steps)

        @block.vector
        def _(dve):
            vec = nc.vector
            for s in B_SEMS["dve"]:
                dve.sem_inc(s, 1)
            vec.memset(kb_t[:, :, 0:WIN], 0.0)
            vec.memset(vb_mid[0:WIN, 0, :], 0.0)
            vec.memset(u_t[E:P, CH - 1, :], 0.0).then_inc(chain_a, 1)
            dve.wait_ge(chain_a, 1)
            vec.memset(u_t[B2ROW:B2ROW + 1, CH - 1, :], 1.0)
            dve.wait_ge(tables_in, 32)
            for l in range(LAYERS):
                for s in range(2):
                    scale = scale_bc[:, l, s, :].unsqueeze(1).broadcast_to([P, NT, E])
                    swapped = scale_bc[:, l, s, :].rearrange("p (h e) -> p h e", h=2)[:, ::-1, :]
                    vec.tensor_tensor(table[:, l, 0, :, s, :], rope[:, 0, :, s, :], scale, ALU.mult)
                    for t in range(NT):
                        last = vec.tensor_tensor(table[:, l, 1, t, s, :].rearrange("p (h e) -> p h e", h=2),
                                                 rope[:, 1, t, s, :].rearrange("p (h e) -> p h e", h=2), swapped, ALU.mult)
            last.then_inc(consts_ready, 2)
            count_a, count_b = [0], [0]

            def link(b, ins):
                count_a[0] += 1
                ins.then_inc(chain_a, 1)
                wait_apart(dve, waited_dve, chain_a, b * CHAIN_A + count_a[0] + 1)

            def link_b(b, ins):
                count_b[0] += 1
                ins.then_inc(chain_b, 1)
                wait_apart(dve, waited_dve, chain_b, b * CHAIN_B + count_b[0] + 1)

            def project(b, r):
                if r == 0:
                    count_a[0] = 0
                for i in range(4 * r + 1, 4 * r + 4, 2):
                    dve.wait_ge(projected, 16 * b + i + 1)
                    if i < 8:
                        last = vec.tensor_scalar(q_t[:, i, :], head_bank(i), E ** -0.5, None, ALU.mult)
                    elif i < 12:
                        last = vec.tensor_copy(k_t[:, i - 8, :], head_bank(i))
                    else:
                        last = vec.tensor_copy(v[:, i - 12, :], head_bank(i))
                    last.then_inc(proj_dve, 1)

            def scores(b, n):
                _, _, w = units_pair(n)
                N = UNITS * b + n
                dve.wait_ge(scored, N + 1)
                vec.tensor_reduce(negmax[:, n % 2, :], a_scores[:, :, 0:w], AX.X, ALU.max, negate=True).then_inc(negmax_ready, 1)
                dve.wait_ge(exp_done, N + 1)
                vec.reciprocal(rowinv[:, n % 2, :], rowsum[:, n % 2, :]).then_inc(rowinv_ready, 1)

            def turn(b, n):
                _, _, w = units_pair(n)
                N = UNITS * b + n
                dve.wait_ge(turned, N + 1)
                need(dve, valued, N - 1)
                vec.tensor_copy(prob_t[:, n % 2, 1, 0:w], a_turned[:, 1, 0:w]).then_inc(prob_t_dve, 1)

            def out_a(b, _):
                dve.wait_ge(out_done, b + 1)
                dve.wait_ge(x_res_ready, b + 1)
                link(b, vec.tensor_tensor(y[:].rearrange("p t d -> p (t d)"), a_turned[:, 0, :],
                                          x_res[:].rearrange("p t d -> p (t d)"), ALU.add))
                for t in range(NT):
                    last = vec.bn_stats(st_a[:, t, :], y[:, t, :])
                link(b, last)
                for t in range(NT):
                    last = vec.bn_aggr(mv_a[:, t, :], st_a[:, t, :])
                last.then_inc(var_a_ready, 1)
                dve.wait_ge(rs_a_ready, b + 1)
                for t in range(NT):
                    last = vec.tensor_scalar(x1[:, t, :], y[:, t, :], mv_a[:, t, 0:1], rs_a[:, t:t + 1],
                                             ALU.subtract, ALU.mult)
                last.then_inc(x1_ready, 1)
                assert count_a[0] == CHAIN_A, count_a

            def qkv(b, l, t):
                T = 8 * b + 4 * l + t
                if l == 0 and t == 0:
                    count_b[0] = 0
                dve.wait_ge(qk_ready, T + 2)
                dve.wait_ge(rsum_ready, T + 1)
                dve.wait_ge(rot_ready, T + 1)
                for s in range(2):
                    cos = table[:, l, 0, t, s, :].unsqueeze(1).broadcast_to([P, HB, E])
                    last = vec.tensor_tensor(r1[:, s, :, :], qk[:, s, :, :], cos, ALU.mult)
                last.then_inc(r1_ready, 1)
                for s in range(2):
                    sin = table[:, l, 1, t, s, :].rearrange("p (h e) -> p h e", h=2).unsqueeze(1)
                    swapped = qk[:, s, :, :].rearrange("p n (h e) -> p n h e", h=2)[:, :, ::-1, :]
                    last = vec.tensor_tensor(r2[:, s, :, :].rearrange("p n (h e) -> p n h e", h=2), swapped,
                                             sin.broadcast_to([P, HB, 2, E // 2]), ALU.mult)
                last.then_inc(r2_ready, 1)
                dve.wait_ge(sq_ready, T + 2)
                dve.wait_ge(floor_ready, T + 1)
                vec.tensor_reduce(ssq[:], sq[:].rearrange("p s h e -> p (s h) e"), AX.X, ALU.add).then_inc(ssq_ready, 1)

            def turn_qk(b, l, t):
                dve.wait_ge(qk_turned, 8 * b + 4 * l + t + 2)
                vec.tensor_copy(kb_t[:, :, WIN + t * P:WIN + (t + 1) * P],
                                b_pair[:, 1, :].rearrange("p (c n) -> p c n", c=CB)).then_inc(kb_ready, 1)

            def b_scores(b, l, t):
                T = 8 * b + 4 * l + t
                dve.wait_ge(b_scored, T + 2)
                vec.tensor_reduce(b_negmax[:], b_pair[:].rearrange("p s (c n) -> p (s c) n", c=CB), AX.X, ALU.max,
                                  negate=True).then_inc(b_negmax_ready, 1)
                dve.wait_ge(b_exp_done, T + 2)
                vec.reciprocal(b_rowinv[:], b_rowsum[:]).then_inc(b_rowinv_ready, 1)

            def b_turn(b, l, t):
                dve.wait_ge(b_turned, 8 * b + 4 * l + t + 2)
                vec.tensor_copy(b_prob_t[:, 1, :, :].rearrange("p c n -> p (c n)"), b_pair[:, 1, :]).then_inc(b_pt_dve, 1)

            def b_wo(b, l, t):
                dve.wait_ge(wo_done, 8 * b + 4 * l + t + 2)
                vec.tensor_tensor(x2[:, t, :], b_pair[:, 0, 0:D], (x1 if l == 0 else x3)[:, t, :], ALU.add).then_inc(x2_ready, 1)

            def norm(b, l, _):
                L = 2 * b + l
                dve.wait_ge(x2_ready, 4 * L + 5)
                dve.wait_ge(shifted, L + 2)
                for t in range(NT):
                    vec.bn_stats(st_b[:, t, 0:6], x2[:, t, 0:E])
                    last = vec.bn_stats(st_b[:, t, 6:12], b_misc[:, t * E:(t + 1) * E])
                link_b(b, last)
                for t in range(NT):
                    last = vec.bn_aggr(mv_b[:, t, :], st_b[:, t, :])
                last.then_inc(var_b_ready, 1)
                dve.wait_ge(rs_b_ready, 3 * b + l + 2)
                for t in range(NT):
                    for src, o in ((x2[:, t, 0:E], 0), (b_misc[:, t * E:(t + 1) * E], E)):
                        last = vec.tensor_scalar(x_hat[:, t, o:o + E], src, mv_b[:, t, 0:1], rs_b[:, t:t + 1],
                                                 ALU.subtract, ALU.mult)
                last.then_inc(x_hat_ready, 1)

            def ffn(b, l, _):
                L = 2 * b + l
                for ch in range(CH):
                    m, k = 2 * ch + 1, MCH[ch]
                    bank = b_misc[:] if m % 3 == 2 else b_pair[:, m % 3, :]
                    dve.wait_ge(w1_done, 6 * L + m + 2)
                    dve.wait_ge(gelu_done, CH * L + ch + 2)
                    vec.scalar_tensor_tensor(out=u_t[0:k, ch, :], in0=bank[0:k, :], scalar=b1[0:k, l, 0, ch:ch + 1],
                                             in1=gelu[0:k, ch % 2, :], op0=ALU.add, op1=ALU.mult).then_inc(u_ready, 1)

            def w2_add(b, l, _):
                L = 2 * b + l
                dve.wait_ge(w2_done, L + 2)
                vec.tensor_tensor(x3[:].rearrange("p t d -> p (t d)"), b_misc[:],
                                  x2[:].rearrange("p t d -> p (t d)"), ALU.add).then_inc(x3_ready, 1)

            def final(b, l, _):
                dve.wait_ge(x3_ready, 2 * b + 3)
                dve.wait_ge(y_stored, 16 * b + 16)
                link_b(b, vec.tensor_tensor(x2[:], x3[:], x1[:], ALU.add))
                for t in range(NT):
                    last = vec.bn_stats(st_b[:, t, 0:6], x2[:, t, :])
                link_b(b, last)
                for t in range(NT):
                    last = vec.bn_aggr(mv_b[:, t, :], st_b[:, t, 0:6])
                last.then_inc(var_b_ready, 1)
                dve.wait_ge(rs_b_ready, 3 * b + 2 + 2)
                for t in range(NT):
                    last = vec.tensor_scalar(y_out[:, t, :], x2[:, t, :], mv_b[:, t, 0:1], rs_b[:, t:t + 1],
                                             ALU.subtract, ALU.mult)
                last.then_inc(y_out_ready, 1)
                assert count_b[0] == CHAIN_B, count_b

            steps = {"a_project": project, "a_scores": scores, "a_turn": turn, "a_out": out_a, "b_qkv": qkv,
                     "b_turn_qk": turn_qk, "b_scores": b_scores, "b_turn_p": b_turn, "b_wo": b_wo, "b_norm": norm,
                     "b_ffn": ffn, "b_w2": w2_add, "b_final": final}
            walk(0, None, steps)
            dve.wait_ge(late_in, 16 * 9)
            dve.wait_ge(consts_ready, 2)
            with dve.Fori(1, B) as b:
                walk(b, b - 1, steps)
            walk(None, B - 1, steps)

        @block.gpsimd
        def _(pool):
            for s in B_SEMS["pool"]:
                pool.sem_inc(s, 1)
            nc.gpsimd.memset(minus_half[:], -0.5).then_inc(half_ready, 1)
            pool.wait_ge(early_in, 16 * 8)
            pool.wait_ge(half_ready, 1)

            def turn_x(b, _):
                pool.wait_ge(x_loaded, 16 * (b + 1))
                need(pool, x1_ready, b)
                nc.gpsimd.tensor_tensor(x_res[:], x_in[:], bout[:].unsqueeze(1).broadcast_to([P, NT, D]),
                                        ALU.add).then_inc(x_res_ready, 1)

            def scores(b, n):
                _, _, w = units_pair(n)
                wait_apart(pool, waited_pool, rowinv_ready, UNITS * b + n + 1)
                for h in range(2):
                    pr = prob[:, n % 2, h, 0:w]
                    last = nc.gpsimd.tensor_scalar(pr, pr, rowinv[:, n % 2, h:h + 1], 1.0, ALU.mult, ALU.mult)
                last.then_inc(prob_ready, 1)

            def qkv(b, l, t):
                T = 8 * b + 4 * l + t
                pool.wait_ge(r2_ready, T + 2)
                nc.gpsimd.tensor_tensor(r1[:], r1[:], r2[:], ALU.add).then_inc(rsum_ready, 1)
                wait_apart(pool, waited_pool, ssq_ready, T + 2)
                nc.gpsimd.tensor_scalar(ssq_floor[:], ssq[:], 1e-24, None, ALU.max).then_inc(floor_ready, 1)
                pool.wait_ge(floor_ready, T + 2)
                nc.gpsimd.tensor_tensor(rnorm[:], ssq_floor[:], minus_half[:], ALU.pow).then_inc(rnorm_ready, 1)
                pool.wait_ge(rsum_ready, T + 2)
                pool.wait_ge(rnorm_ready, T + 2)
                pool.wait_ge(qk_turned, T + 1)
                nc.gpsimd.tensor_tensor(rot[:].rearrange("p s h e -> p (s h) e"), r1[:].rearrange("p s h e -> p (s h) e"),
                                        rnorm[:].unsqueeze(2).broadcast_to([P, 2 * HB, E]), ALU.mult).then_inc(rot_ready, 1)

            def b_scores(b, l, t):
                pool.wait_ge(b_rowinv_ready, 8 * b + 4 * l + t + 2)
                pr = b_prob[:].rearrange("p s c n -> p (s c) n")
                nc.gpsimd.tensor_tensor(pr, pr, b_rowinv[:].unsqueeze(2).broadcast_to([P, HB, P]),
                                        ALU.mult).then_inc(b_prob_ready, 1)

            def out_a(b, _):
                wait_apart(pool, waited_pool, var_a_ready, b + 1)
                nc.gpsimd.tensor_scalar(ve_a[:], mv_a[:, :, 1], EPS, None, ALU.add).then_inc(eps_a_ready, 1)
                pool.wait_ge(eps_a_ready, b + 1)
                nc.gpsimd.tensor_tensor(rs_a[:], ve_a[:], minus_half[:, 0:NT], ALU.pow).then_inc(rs_a_ready, 1)

            def inverse_deviation(b, k):
                wait_apart(pool, waited_pool, var_b_ready, 3 * b + k + 2)
                nc.gpsimd.tensor_scalar(ve_b[:], mv_b[:, :, 1], EPS, None, ALU.add).then_inc(eps_b_ready, 1)
                pool.wait_ge(eps_b_ready, 3 * b + k + 2)
                nc.gpsimd.tensor_tensor(rs_b[:], ve_b[:], minus_half[:, 0:NT], ALU.pow).then_inc(rs_b_ready, 1)

            def norm(b, l, _):
                inverse_deviation(b, l)

            def final(b, l, _):
                inverse_deviation(b, LAYERS)

            all_sequences(pool, {"a_out": out_a, "b_norm": norm, "b_final": final, "a_turn_x": turn_x, "a_scores": scores, "b_qkv": qkv, "b_scores": b_scores})


def constants():
    bf = mybir.dt.np(BF16)
    i = np.arange(P)
    q, k = i[:, None], i[None, :]
    causal = np.where(k > q, MASKED, 0.0)
    qw = (i % WIN)[:, None]
    seen = (k >= qw) & (k <= qw + WIN)
    first = seen & ((k >= WIN) | (q >= WIN))
    band = np.stack([np.where(first, 0.0, MASKED), np.where(seen, 0.0, MASKED)], 1)
    half = np.arange(0, E, 2, dtype=np.float32)
    inv_freq = (np.float32(1.0) / np.float32(10000.0) ** (half / np.float32(E))).astype(np.float32)
    t = np.arange(S, dtype=np.float32)
    freqs = t[:, None] * inv_freq[None, :]
    base = (half + np.float32(0.4 * E)) / np.float32(1.4 * E)
    power = (t - S // 2) / np.float32(WIN // 2)
    scale = (base[None, :] ** power[:, None]).astype(np.float32)
    cos, sin = np.cos(freqs), np.sin(freqs)
    rope = np.zeros((2, S, 2, E), np.float32)
    for s, f in enumerate((scale * np.float32(8.0), np.float32(1.0) / scale)):
        rope[0, :, s, :] = np.concatenate([cos * f, cos * f], 1)
        rope[1, :, s, :] = np.concatenate([-sin * f, sin * f], 1)
    rope = rope.reshape(2, NT, P, 2, E).transpose(2, 0, 1, 3, 4)
    last = np.zeros((P, P))
    last[P - 1, 0] = 1.0
    return {
        "ident": np.eye(P, dtype=np.float32), "ident_b": np.eye(P).astype(bf), "causal": causal.astype(bf),
        "band": band.astype(bf), "shift_m": np.eye(P, k=1, dtype=np.float32), "last_m": last.astype(np.float32),
        "rope": np.ascontiguousarray(rope),
    }


def kernel(**inputs):
    import numpy as _np
    import concourse.bacc as _bacc
    from concourse import mybir as _mybir
    from concourse.bass_utils import run_bass_kernel_spmd as _run

    a = {k: _np.asarray(v) for k, v in inputs.items()}
    c = _np.ascontiguousarray
    arrays = constants()
    x = a["L0_attn_resid"]
    arrays["x"] = c(x)
    arrays["wq"] = c(a["L0_attn_W_Q"].reshape(D, 4, 2, 2, E).transpose(0, 1, 3, 2, 4).reshape(D, CA, P))
    arrays["wk"] = c(a["L0_attn_W_K"].reshape(D, GA // 2, P))
    arrays["wv"] = c(a["L0_attn_W_V"].reshape(D, GA * E))
    arrays["wout"] = c(a["L0_attn_W_out"].reshape(E, 4, 2, 2, D).transpose(2, 0, 1, 3, 4).reshape(P, CA, D))
    arrays["bout"] = c(a["L0_attn_b_out"])
    arrays["scales"] = c(_np.stack([a["L0_ffn_q_scale"], a["L0_ffn_k_scale"]], 1))
    arrays["wqkv"] = c(a["L0_ffn_wqkv"].transpose(1, 0, 2))
    arrays["wo"] = c(a["L0_ffn_wo"].reshape(LAYERS, CB, P, D).transpose(2, 0, 1, 3))
    arrays["w1"] = c(a["L0_ffn_w1"].transpose(1, 0, 2))
    w2 = _np.zeros((LAYERS, CH * P, D), _np.float32)
    w2[:, :HID] = a["L0_ffn_w2"]
    w2[:, 2 * P + B2ROW] = a["L0_ffn_b2"]
    arrays["w2"] = c(w2.reshape(LAYERS, CH, P, D).transpose(2, 0, 1, 3))
    b1 = _np.zeros((LAYERS, 2, CH * P), _np.float32)
    b1[:, :, :HID] = a["L0_ffn_b1"].reshape(LAYERS, 2, HID)
    arrays["b1"] = c(b1.reshape(LAYERS, 2, CH, P).transpose(3, 0, 1, 2))
    arrays["ln_gb"] = c(_np.stack([a["L0_ffn_ln_g"], a["L0_ffn_ln_b"]], 1).transpose(2, 0, 1))

    nc = _bacc.Bacc("TRN2", target_bir_lowering=False, num_devices=1)
    feed, t_in = {}, {}
    for name, arr in arrays.items():
        feed[f"in_{name}"] = arr
        t_in[name] = nc.dram_tensor(f"in_{name}", arr.shape, _mybir.dt.from_np(arr.dtype), kind="ExternalInput").ap()
    out = nc.dram_tensor("out_0", (B, S, D), F32, kind="ExternalOutput").ap()
    program(nc, t_in, out)
    r = _run(nc, [feed], core_ids=[0])
    return r.results[0]["out_0"]
```

```python
from contextlib import ExitStack

import numpy as np

import concourse.bass as bass
from concourse import mybir
from concourse.alu_op_type import AluOpType as ALU

ACT = mybir.ActivationFunctionType
AX = mybir.AxisListType
F32 = mybir.dt.float32
BF16 = mybir.dt.bfloat16

P = 128
B, S, D = 8, 512, 128
NT = S // P
E = 64
HA, GA = 16, 8
CA = HA // 2
UNITS = CA * NT
LAYERS, HB = 2, 8
CB = HB // 2
WIN = 64
INNER = HB * E
HID = 341
CH = 3
MCH = [128, 128, HID - 256]
EPS = 1e-5
B2ROW = 96
MASKED = -1e30


def stream_a(beside_b):
    last = UNITS - 1
    copy = lambda r: [("act", "a_project", r), ("dve", "a_project", r)]
    out = [("a_turn_x", (0,), {"sp": (60, []), "pe": (500, [("sp", "a_turn_x", 0)]), "act": (600, [("pe", "a_turn_x", 0)]),
                               "pool": (1300, [("sp", "a_turn_x", 0)])})]
    for r in range(4):
        before = copy(r - 1) if r else [("act", "a_turn_x", 0)]
        out.append(("a_project", (r,), {"pe": (3500, before), "act": (1000, [("pe", "a_project", r)]),
                                        "dve": (1200, [("pe", "a_project", r)])}))

    def scores(n):
        w = P * (n % NT + 1)
        before = copy(3) if n == 0 else [("act", "a_scores", n - 1)]
        return ("a_scores", (n,), {"pe": (3.4 * w + 150, before), "dve": (2.1 * w + 100, [("pe", "a_scores", n)]),
                                   "act": (1.67 * w + 500, [("dve", "a_scores", n)])})

    def inverse(n):
        w = P * (n % NT + 1)
        return ("a_inverse", (n,), {"dve": (80, [("act", "a_scores", n)]),
                                    "pool": (1.67 * w + 500, [("dve", "a_inverse", n)])})

    def turn(n):
        w = P * (n % NT + 1)
        return ("a_turn", (n,), {"pe": (1.7 * w, [("pool", "a_inverse", n)] + [(e, "a_turn", n - 1) for e in ("act", "dve") if n]),
                                 "act": (0.83 * w + 60, [("pe", "a_turn", n)]),
                                 "dve": (1.04 * w + 70, [("pe", "a_turn", n)])})

    def value(n):
        i = n % NT
        before = [("act", "a_turn", n), ("dve", "a_turn", n)] + ([("act", "a_value", n - 1)] if i == 0 and n else [])
        parts = {"pe": (270 * (i + 1), before)}
        if i == NT - 1:
            parts["act"] = (500, [("pe", "a_value", n)])
        return ("a_value", (n,), parts)

    out += [scores(0), inverse(0)]
    for n in range(UNITS):
        out += ([scores(n + 1)] if n < last else []) + ([value(n - 1)] if n else []) + [turn(n)]
        out += [inverse(n + 1)] if n < last else []
    out += [value(last)]
    out.append(("a_out", (0,), {"pe": (7000, [("act", "a_value", last)]), "dve": (2000, [("pe", "a_out", 0)])}))
    out.append(("a_deviation", (0,), {"pool": (1700, [("dve", "a_out", 0)])}))
    read = [("dve", "b_end_stats", (LAYERS, 0))] if beside_b else []
    out.append(("a_norm", (0,), {"dve": (900, [("pool", "a_deviation", 0)] + read)}))
    return out


def stream_b():
    out = []
    for l in range(LAYERS):
        def qkv(t):
            before = [("act", "b_turn_qk", (l, t - 1)), ("dve", "b_turn_qk", (l, t - 1))] if t else [("act", "b_shift", (l, 0))]
            return ("b_qkv", (l, t), {"pe": (2600, before), "act": (2400, [("pe", "b_qkv", (l, t))]),
                                      "sp": (2000, [("act", "b_qkv", (l, t))])})

        def rotate(t):
            return ("b_rotate", (l, t), {"dve": (2400, [("act", "b_qkv", (l, t))])})

        def lengths(t):
            return ("b_lengths", (l, t), {"dve": (2300, [("act", "b_qkv", (l, t))]),
                                          "pool": (5000, [("dve", "b_lengths", (l, t))])})

        def turn_qk(t):
            return ("b_turn_qk", (l, t), {"pe": (900, [("pool", "b_lengths", (l, t))]), "act": (500, [("pe", "b_turn_qk", (l, t))]),
                                          "dve": (600, [("pe", "b_turn_qk", (l, t))])})

        out += [("b_shift", (l, 0), {"pe": (1500, [("dve", "b_w2", (l - 1, 0))] if l else []),
                                     "act": (500, [("pe", "b_shift", (l, 0))])}),
                qkv(0), rotate(0), lengths(0), turn_qk(0)]
        for t in range(NT):
            k = (l, t)
            out += [qkv(t + 1)] if t + 1 < NT else []
            out.append(("b_scores", k, {"pe": (2500, [("act", "b_qkv", (l, t + 1))] if t + 1 < NT else [("dve", "b_turn_qk", k)]),
                                        "dve": (1150, [("pe", "b_scores", k)]), "act": (2800, [("dve", "b_scores", k)])}))
            out += [rotate(t + 1)] if t + 1 < NT else []
            out.append(("b_inverse", k, {"dve": (150, [("act", "b_scores", k)]), "pool": (1900, [("dve", "b_inverse", k)])}))
            out += [lengths(t + 1)] if t + 1 < NT else []
            out.append(("b_turn_p", k, {"pe": (900, [("pool", "b_inverse", k)]), "act": (500, [("pe", "b_turn_p", k)]),
                                        "dve": (600, [("pe", "b_turn_p", k)])}))
            out.append(("b_value", k, {"pe": (1600, [("act", "b_turn_p", k), ("dve", "b_turn_p", k), ("sp", "b_qkv", k)]),
                                       "act": (500, [("pe", "b_value", k)])}))
            out.append(("b_wo", k, {"pe": (900, [("act", "b_value", k)]), "dve": (200, [("pe", "b_wo", k)])}))
            out += [turn_qk(t + 1)] if t + 1 < NT else []
        k = (l, 0)
        out.append(("b_stats", k, {"pe": (1700, [("dve", "b_wo", (l, NT - 1))]), "dve": (1700, [("pe", "b_stats", k)])}))
        out.append(("b_deviation", k, {"pool": (1700, [("dve", "b_stats", k)])}))
        out.append(("b_norm", k, {"dve": (1500, [("pool", "b_deviation", k)])}))
        out.append(("b_turn_f", k, {"pe": (450, [("dve", "b_norm", k)]), "act": (650, [("pe", "b_turn_f", k)])}))
        for m in range(2 * CH):
            before = {0: [("act", "b_turn_f", k)], 3: [("act", "b_ffn", (l, 0))], 4: [("dve", "b_ffn", (l, 1))],
                      5: [("act", "b_ffn", (l, 2))]}.get(m, [])
            parts = {"pe": (860, before)}
            if m % 2:
                parts["dve"] = (600, [("pe", "b_ffn", (l, m)), ("act", "b_ffn", (l, m - 1))])
            else:
                parts["act"] = (600, [("pe", "b_ffn", (l, m))])
            out.append(("b_ffn", (l, m), parts))
        out.append(("b_w2", k, {"pe": (2700, [("dve", "b_ffn", (l, 2 * CH - 1))]), "dve": (600, [("pe", "b_w2", k)])}))
    k = (LAYERS, 0)
    out.append(("b_end_stats", k, {"dve": (1700, [("dve", "b_w2", (LAYERS - 1, 0))])}))
    out.append(("b_deviation", k, {"pool": (1700, [("dve", "b_end_stats", k)])}))
    out.append(("b_end", k, {"dve": (900, [("pool", "b_deviation", k)]), "sp": (60, [("dve", "b_end", k)])}))
    return out


ENGINES = ("pe", "act", "dve", "pool", "sp")
SIGNAL_NS = 250


def merge(streams):
    queue = {(e, k): [(name, args, *parts[e]) for name, args, parts in s if e in parts]
             for k, s in enumerate(streams) for e in ENGINES}
    free, done, order = dict.fromkeys(ENGINES, 0.0), {}, {e: [] for e in ENGINES}
    while any(queue.values()):
        heads = []
        for (e, k), q in queue.items():
            if q:
                before = [(x, name, a if isinstance(a, tuple) else (a,)) for x, name, a in q[0][3]]
                if all(x in done for x in before):
                    ready = max([done[x] + SIGNAL_NS for x in before], default=0.0)
                    heads.append((max(free[e], ready), -k, e, k))
        start, _, e, k = min(heads)
        name, args, ns, _ = queue[e, k].pop(0)
        free[e] = done[e, name, args] = start + ns
        order[e].append((name, args))
    return order


BOTH, ONLY_A, ONLY_B = merge([stream_a(True), stream_b()]), merge([stream_a(False)]), merge([stream_b()])
CHAIN_A, CHAIN_B = 2, 4


def program(nc, t_in, out):
    ctx = ExitStack()
    with ctx:
        def sb(name, shape, dt=F32):
            return ctx.enter_context(nc.sbuf_tensor(name, shape, dt))

        def ps(name, shape):
            return ctx.enter_context(nc.psum_tensor(name, shape, F32))

        def sem(name):
            return ctx.enter_context(nc.semaphore(name))

        ident, ident_b = sb("ident", [P, P]), sb("ident_b", [P, P], BF16)
        causal = sb("causal", [P, P], BF16)
        band = sb("band", [P, 2, P], BF16)
        shift_m, last_m = sb("shift_m", [P, P]), sb("last_m", [P, P])
        rope = sb("rope", [P, 2, NT, 2, E])
        scale_bc = sb("scale_bc", [P, LAYERS, 2, E])
        table = sb("table", [P, LAYERS, 2, NT, 2, E])
        wq, wk, wv = sb("wq", [P, CA, P]), sb("wk", [P, GA // 2, P]), sb("wv", [P, GA * E])
        wout, bout = sb("wout", [P, CA, D]), sb("bout", [P, D])
        wqkv, wo = sb("wqkv", [P, LAYERS, 3 * INNER]), sb("wo", [P, LAYERS, CB, D])
        w1, w2 = sb("w1", [P, LAYERS, 2 * HID]), sb("w2", [P, LAYERS, CH, D])
        b1 = sb("b1", [P, LAYERS, 2, CH])
        ln_gb = sb("ln_gb", [P, LAYERS, 2])
        x_in, x_res, x_t = sb("x_in", [P, NT, D]), sb("x_res", [P, NT, D]), sb("x_t", [P, S])
        q_t, k_t, v = sb("q_t", [P, CA, S]), sb("k_t", [P, GA // 2, S]), sb("v", [P, NT, GA * E])
        negmax, rowsum, rowinv = sb("negmax", [P, 2, 2]), sb("rowsum", [P, 2, 2]), sb("rowinv", [P, 2, 2])
        prob, prob_t = sb("prob", [P, 2, 2, S]), sb("prob_t", [P, 2, 2, S])
        z_t, y = sb("z_t", [P, CA, S]), sb("y", [P, NT, D])
        st_a, mv_a, ve_a, rs_a = sb("st_a", [P, NT, 6]), sb("mv_a", [P, NT, 2]), sb("ve_a", [P, NT]), sb("rs_a", [P, NT])
        x1 = sb("x1", [P, NT, D])
        h_t = sb("h_t", [P, S])
        qk, sq = sb("qk", [P, 2, HB, E]), sb("sq", [P, 2, HB, E])
        r1, r2, rot = sb("r1", [P, 2, HB, E]), sb("r2", [P, 2, HB, E]), sb("rot", [P, 2, HB, E])
        ssq, ssq_floor, rnorm = sb("ssq", [P, 2 * HB]), sb("ssq_floor", [P, 2 * HB]), sb("rnorm", [P, 2 * HB])
        minus_half = sb("minus_half", [P, 2 * HB])
        qb_t, kb_t = sb("qb_t", [P, CB, P]), sb("kb_t", [P, CB, WIN + S])
        vb, vb_mid = sb("vb", [P, NT, INNER]), sb("vb_mid", [P, NT, INNER])
        b_negmax, b_rowsum, b_rowinv = sb("b_negmax", [P, HB]), sb("b_rowsum", [P, HB]), sb("b_rowinv", [P, HB])
        b_prob, b_prob_t = sb("b_prob", [P, 2, CB, P]), sb("b_prob_t", [P, 2, CB, P])
        o_t = sb("o_t", [P, CB, P])
        x2, x3 = sb("x2", [P, NT, D]), sb("x3", [P, NT, D])
        st_b, mv_b, ve_b, rs_b = sb("st_b", [P, NT, 12]), sb("mv_b", [P, NT, 2]), sb("ve_b", [P, NT]), sb("rs_b", [P, NT])
        x_hat, f_t = sb("x_hat", [P, NT, D]), sb("f_t", [P, S])
        gelu, u_t = sb("gelu", [P, 2, S]), sb("u_t", [P, CH, S])
        y_out = sb("y_out", [P, NT, D])

        a_scores, a_turned, a_z = ps("a_scores", [P, 2, 512]), ps("a_turned", [P, 2, 512]), ps("a_z", [P, 512])
        b_pair, b_misc = ps("b_pair", [P, 2, 512]), ps("b_misc", [P, 512])

        early_in, late_in, tables_in = sem("early_in"), sem("late_in"), sem("tables_in")
        consts_ready = sem("consts_ready")
        x_loaded, x_turned, x_t_ready, x_res_ready = sem("x_loaded"), sem("x_turned"), sem("x_t_ready"), sem("x_res_ready")
        projected, proj_act, proj_dve = sem("projected"), sem("proj_act"), sem("proj_dve")
        scored, negmax_ready, exp_done = sem("scored"), sem("negmax_ready"), sem("exp_done")
        rowinv_ready, prob_ready, turned = sem("rowinv_ready"), sem("prob_ready"), sem("turned")
        prob_t_act, prob_t_dve, valued, z_ready = sem("prob_t_act"), sem("prob_t_dve"), sem("valued"), sem("z_ready")
        out_done, chain_a, x1_ready = sem("out_done"), sem("chain_a"), sem("x1_ready")
        var_a_ready, eps_a_ready, rs_a_ready = sem("var_a_ready"), sem("eps_a_ready"), sem("rs_a_ready")
        half_ready = sem("half_ready")
        B_SEMS = {}

        def bsem(name, engine):
            s = sem(name)
            B_SEMS.setdefault(engine, []).append(s)
            return s

        h_done, h_ready = bsem("h_done", "pe"), bsem("h_ready", "act")
        qkv_done, qk_ready, vb_ready = bsem("qkv_done", "pe"), bsem("qk_ready", "act"), bsem("vb_ready", "act")
        sq_ready, r1_ready, r2_ready = bsem("sq_ready", "act"), bsem("r1_ready", "dve"), bsem("r2_ready", "dve")
        ssq_ready, floor_ready, rnorm_ready = bsem("ssq_ready", "dve"), bsem("floor_ready", "pool"), bsem("rnorm_ready", "pool")
        var_b_ready, eps_b_ready, rs_b_ready = bsem("var_b_ready", "dve"), bsem("eps_b_ready", "pool"), bsem("rs_b_ready", "pool")
        rsum_ready, rot_ready, qk_turned = bsem("rsum_ready", "dve"), bsem("rot_ready", "pool"), bsem("qk_turned", "pe")
        qb_ready, kb_ready = bsem("qb_ready", "act"), bsem("kb_ready", "dve")
        b_scored, b_negmax_ready, b_exp_done = bsem("b_scored", "pe"), bsem("b_negmax_ready", "dve"), bsem("b_exp_done", "act")
        b_rowinv_ready, b_prob_ready, b_turned = bsem("b_rowinv_ready", "dve"), bsem("b_prob_ready", "pool"), bsem("b_turned", "pe")
        b_pt_act, b_pt_dve = bsem("b_pt_act", "act"), bsem("b_pt_dve", "dve")
        b_valued, o_ready, wo_done, x2_ready = bsem("b_valued", "pe"), bsem("o_ready", "act"), bsem("wo_done", "pe"), bsem("x2_ready", "dve")
        shifted, chain_b, x_hat_ready = bsem("shifted", "pe"), bsem("chain_b", "dve"), bsem("x_hat_ready", "dve")
        f_turned, f_ready, w1_done = bsem("f_turned", "pe"), bsem("f_ready", "act"), bsem("w1_done", "pe")
        gelu_done, u_ready, w2_done, x3_ready = bsem("gelu_done", "act"), bsem("u_ready", "dve"), bsem("w2_done", "pe"), bsem("x3_ready", "dve")
        y_out_ready = bsem("y_out_ready", "dve")
        y_stored = sem("y_stored")
        v_hi = [sem(f"v_hi{t}") for t in range(NT)]
        v_lo = [sem(f"v_lo{t}") for t in range(NT)]

        def head_bank(i):
            return (a_scores if i % 4 < 2 else a_turned)[:, i % 2, :]

        def units_pair(n):
            return n // NT, n % NT, P * (n % NT + 1)

        def walk(order, a_index, b_index, steps):
            for name, args in order:
                if name in steps:
                    steps[name](a_index if name[0] == "a" else b_index, *args)

        def all_sequences(eng, engine, steps, between=()):
            walk(ONLY_A[engine], 0, None, steps)
            for s, value in between:
                eng.wait_ge(s, value)
            with eng.Fori(1, B) as b:
                walk(BOTH[engine], b, b - 1, steps)
            walk(ONLY_B[engine], None, B - 1, steps)

        def need(eng, s, value):
            if not (type(value) is int and value <= 0):
                eng.wait_ge(s, value)

        waited_dve, waited_pool = sem("waited_dve"), sem("waited_pool")

        def wait_apart(eng, passed, s, value):
            eng.wait_ge(s, value)
            eng.sem_inc(passed, 1)

        block = ctx.enter_context(nc.Block())

        @block.sync
        def _(sp):
            for dst, src in ((ident, "ident"), (causal, "causal"), (ident_b, "ident_b"), (wq, "wq"), (wk, "wk"),
                             (wv, "wv"), (wout, "wout")):
                sp.dma_start(dst[:], t_in[src]).then_inc(early_in, 16)
            sp.dma_start(bout[:], t_in["bout"].partition_broadcast(P)).then_inc(early_in, 16)
            sp.sem_inc(y_stored, 16)

            def load(b, _):
                need(sp, x_turned, b)
                need(sp, x_res_ready, b)
                src = t_in["x"][b] if type(b) is int else t_in["x"][bass.ds(b, 1)].rearrange("o s d -> (o s) d")
                sp.dma_start(x_in[:], src.rearrange("(t p) d -> p t d", p=P)).then_inc(x_loaded, 16)

            load(0, 0)
            sp.dma_start(rope[:], t_in["rope"]).then_inc(tables_in, 16)
            sp.dma_start(scale_bc[:], t_in["scales"].partition_broadcast(P)).then_inc(tables_in, 16)
            for dst, src in ((band, "band"), (shift_m, "shift_m"), (last_m, "last_m"), (wqkv, "wqkv"), (wo, "wo"),
                             (w1, "w1"), (w2, "w2"), (b1, "b1"), (ln_gb, "ln_gb")):
                sp.dma_start(dst[:], t_in[src]).then_inc(late_in, 16)

            def v_shift(b, l, t):
                sp.wait_ge(vb_ready, 8 * b + 4 * l + t + 2)
                sp.dma_start(vb_mid[WIN:P, t, :], vb[0:WIN, t, :]).then_inc(v_hi[t], 16)
                if t + 1 < NT:
                    sp.dma_start(vb_mid[0:WIN, t + 1, :], vb[WIN:P, t, :]).then_inc(v_lo[t + 1], 16)

            def store(b, l, _):
                sp.wait_ge(y_out_ready, b + 2)
                if type(b) is int:
                    dst = out[b]
                else:
                    dst = out[bass.ds(b, 1)].rearrange("o s d -> (o s) d")
                sp.dma_start(dst.rearrange("(t p) d -> p t d", p=P), y_out[:]).then_inc(y_stored, 16)

            steps = {"a_turn_x": load, "b_qkv": v_shift, "b_end": store}
            with sp.Fori(1, B) as b:
                walk(BOTH["sp"], b, b - 1, steps)
            walk(ONLY_B["sp"], None, B - 1, steps)
            sp.wait_ge(y_stored, 16 * (B + 1))

        @block.tensor
        def _(pe):
            for s in B_SEMS["pe"]:
                pe.sem_inc(s, 1)
            pe.wait_ge(early_in, 16 * 8)
            mm = nc.tensor.matmul

            def turn_x(b, _):
                pe.wait_ge(x_loaded, 16 * (b + 1))
                need(pe, prob_t_dve, UNITS * b)
                for t in range(NT):
                    last = nc.tensor.transpose(a_turned[:, 1, t * P:(t + 1) * P], x_in[:, t, :], ident[:])
                last.then_inc(x_turned, 1)

            def project(b, r):
                for i in range(4 * r, 4 * r + 4):
                    if i == 0:
                        pe.wait_ge(x_t_ready, b + 1)
                        need(pe, exp_done, UNITS * b)
                        need(pe, x1_ready, b)
                    if i >= 4:
                        pe.wait_ge(proj_dve if i % 2 else proj_act, 8 * b + i // 2 - 1)
                    if i < 8:
                        last = mm(head_bank(i), wq[:, i, :], x_t[:], start=True, stop=True)
                    elif i < 12:
                        last = mm(head_bank(i), wk[:, i - 8, :], x_t[:], start=True, stop=True)
                    else:
                        last = mm(head_bank(i), x_t[:, (i - 12) * P:(i - 11) * P], wv[:], start=True, stop=True)
                    last.then_inc(projected, 1)

            def scores(b, n):
                c, i, w = units_pair(n)
                if n == 0:
                    pe.wait_ge(proj_act, 8 * b + 8)
                    pe.wait_ge(proj_dve, 8 * b + 8)
                else:
                    pe.wait_ge(exp_done, UNITS * b + n)
                for h in range(2):
                    half = slice(E * h, E * h + E)
                    mm(a_scores[:, h, 0:w], q_t[half, c, i * P:(i + 1) * P], k_t[half, c // 2, 0:w],
                       start=True, stop=False)
                for h in range(2):
                    last = mm(a_scores[:, h, w - P:w], ident_b[:], causal[:], start=False, stop=True)
                last.then_inc(scored, 1)

            def turn(b, n):
                _, i, _ = units_pair(n)
                pe.wait_ge(prob_ready, UNITS * b + n + 1)
                if n:
                    pe.wait_ge(prob_t_act, UNITS * b + n)
                    pe.wait_ge(prob_t_dve, UNITS * b + n)
                for h in range(2):
                    for j in range(i + 1):
                        last = nc.tensor.transpose(a_turned[:, h, j * P:(j + 1) * P],
                                                   prob[:, n % 2, h, j * P:(j + 1) * P], ident[:])
                last.then_inc(turned, 1)

            def value(b, n):
                c, i, _ = units_pair(n)
                pe.wait_ge(prob_t_act, UNITS * b + n + 1)
                pe.wait_ge(prob_t_dve, UNITS * b + n + 1)
                if i == 0:
                    need(pe, z_ready, CA * b + c)
                for j in range(i + 1):
                    for h in range(2):
                        g = 2 * (c // 2) + h
                        last = mm(a_z[E * h:E * h + E, i * P:(i + 1) * P], v[:, j, g * E:(g + 1) * E],
                                  prob_t[:, n % 2, h, j * P:(j + 1) * P], start=(j == 0), stop=(j == i))
                last.then_inc(valued, 1)

            def out_a(b, _):
                pe.wait_ge(z_ready, CA * b + CA)
                for t in range(NT):
                    for c in range(CA):
                        last = mm(a_turned[:, 0, t * P:(t + 1) * P], z_t[:, c, t * P:(t + 1) * P], wout[:, c, :],
                                  start=(c == 0), stop=(c == CA - 1))
                last.then_inc(out_done, 1)

            def shift(b, l, _):
                src = x1 if l == 0 else x3
                if l == 0:
                    pe.wait_ge(x1_ready, b + 1)
                pe.wait_ge(x3_ready, 2 * b + l + 1)
                for t in range(NT):
                    cols = slice(t * P, (t + 1) * P)
                    mm(b_misc[0:E, cols], src[:, t, 0:E], ident[:], start=True, stop=True)
                    last = mm(b_misc[E:P, cols], src[:, t, E:P], shift_m[:], start=True, stop=(t == 0))
                    if t:
                        last = mm(b_misc[E:P, cols], src[:, t - 1, E:P], last_m[:], start=False, stop=True)
                last.then_inc(h_done, 1)

            def qkv(b, l, t):
                T = 8 * b + 4 * l + t
                if t == 0:
                    pe.wait_ge(h_ready, 2 * b + l + 2)
                    pe.wait_ge(u_ready, CH * (2 * b + l) + 1)
                else:
                    pe.wait_ge(qb_ready, T + 1)
                    pe.wait_ge(kb_ready, T + 1)
                    pe.wait_ge(o_ready, T)
                lhs = h_t[:, t * P:(t + 1) * P]
                mm(b_pair[:, 0, :], lhs, wqkv[:, l, 0:INNER], start=True, stop=True)
                mm(b_pair[:, 1, :], lhs, wqkv[:, l, INNER:2 * INNER], start=True, stop=True)
                mm(b_misc[:], lhs, wqkv[:, l, 2 * INNER:], start=True, stop=True).then_inc(qkv_done, 1)

            def turn_qk(b, l, t):
                T = 8 * b + 4 * l + t
                pe.wait_ge(rot_ready, T + 2)
                pe.wait_ge(x2_ready, T + 1)
                for s in range(2):
                    for c in range(CB):
                        last = nc.tensor.transpose(b_pair[:, s, c * P:(c + 1) * P],
                                                   rot[:, s, 2 * c:2 * c + 2, :].rearrange("p h e -> p (h e)"), ident[:])
                last.then_inc(qk_turned, 1)

            def b_score(b, l, t):
                T = 8 * b + 4 * l + t
                pe.wait_ge(qb_ready, T + 2)
                pe.wait_ge(kb_ready, T + 2)
                if t + 1 < NT:
                    pe.wait_ge(qk_ready, T + 3)
                for s in range(2):
                    mm(b_pair[:, s, :], ident_b[:],
                       band[:, min(t, 1), :].unsqueeze(1).broadcast_to([P, CB, P]), start=True, stop=True)
                for c in range(CB):
                    for w in range(2):
                        for s in range(2):
                            half = slice(E * s, E * s + E)
                            k0 = t * P + WIN * w
                            last = mm(b_pair[WIN * w:WIN * w + WIN, s, c * P:(c + 1) * P],
                                      qb_t[half, c, WIN * w:WIN * w + WIN], kb_t[half, c, k0:k0 + P],
                                      start=False, stop=True, skip_group_check=True)
                last.then_inc(b_scored, 1)

            def b_turn(b, l, t):
                pe.wait_ge(b_prob_ready, 8 * b + 4 * l + t + 2)
                for s in range(2):
                    for c in range(CB):
                        last = nc.tensor.transpose(b_pair[:, s, c * P:(c + 1) * P], b_prob[:, s, c, :], ident[:])
                last.then_inc(b_turned, 1)

            def b_value(b, l, t):
                T = 8 * b + 4 * l + t
                pe.wait_ge(b_pt_act, T + 2)
                pe.wait_ge(b_pt_dve, T + 2)
                pe.wait_ge(v_hi[t], 16 * (2 * b + l) + 16)
                if t:
                    pe.wait_ge(v_lo[t], 16 * (2 * b + l) + 16)
                if t + 1 < NT:
                    pe.wait_ge(vb_ready, T + 3)
                for c in range(CB):
                    for w in range(2):
                        for s in range(2):
                            h = 2 * c + s
                            src = vb if w else vb_mid
                            last = mm(b_misc[E * s:E * s + E, c * P + WIN * w:c * P + WIN * w + WIN],
                                      src[:, t, h * E:(h + 1) * E], b_prob_t[:, s, c, WIN * w:WIN * w + WIN],
                                      start=True, stop=True)
                last.then_inc(b_valued, 1)

            def b_wo(b, l, t):
                pe.wait_ge(o_ready, 8 * b + 4 * l + t + 2)
                for c in range(CB):
                    last = mm(b_pair[:, 0, 0:D], o_t[:, c, :], wo[:, l, c, :], start=(c == 0), stop=(c == CB - 1))
                last.then_inc(wo_done, 1)

            def norm(b, l, _):
                pe.wait_ge(x2_ready, 8 * b + 4 * l + 5)
                for t in range(NT):
                    cols = slice(t * E, (t + 1) * E)
                    last = mm(b_misc[:, cols], shift_m[:], x2[:, t, E:P], start=True, stop=(t == 0))
                    if t:
                        last = mm(b_misc[:, cols], last_m[:], x2[:, t - 1, E:P], start=False, stop=True)
                last.then_inc(shifted, 1)

            def turn_f(b, l, _):
                pe.wait_ge(x_hat_ready, 2 * b + l + 2)
                for t in range(NT):
                    last = nc.tensor.transpose(b_misc[:, t * P:(t + 1) * P], x_hat[:, t, :], ident[:])
                last.then_inc(f_turned, 1)

            def ffn(b, l, m):
                L = 2 * b + l
                ch, part = m // 2, 1 - m % 2
                if m == 0:
                    pe.wait_ge(f_ready, L + 2)
                if m in (3, 5):
                    pe.wait_ge(gelu_done, CH * L + (2 if m == 3 else 3))
                if m == 4:
                    pe.wait_ge(u_ready, CH * L + 2)
                bank = b_misc[:] if m % 3 == 2 else b_pair[:, m % 3, :]
                o = part * HID + ch * P
                mm(bank[0:MCH[ch], :], w1[:, l, o:o + MCH[ch]], f_t[:], start=True, stop=True).then_inc(w1_done, 1)

            def w2_mul(b, l, _):
                L = 2 * b + l
                pe.wait_ge(u_ready, CH * L + CH + 1)
                for t in range(NT):
                    for ch in range(CH):
                        last = mm(b_misc[:, t * P:(t + 1) * P], u_t[:, ch, t * P:(t + 1) * P], w2[:, l, ch, :],
                                  start=(ch == 0), stop=(ch == CH - 1))
                last.then_inc(w2_done, 1)

            steps = {"a_turn_x": turn_x, "a_project": project, "a_scores": scores, "a_turn": turn, "a_value": value,
                     "a_out": out_a, "b_shift": shift, "b_qkv": qkv, "b_turn_qk": turn_qk, "b_scores": b_score,
                     "b_turn_p": b_turn, "b_value": b_value, "b_wo": b_wo, "b_stats": norm, "b_turn_f": turn_f,
                     "b_ffn": ffn, "b_w2": w2_mul}
            all_sequences(pe, "pe", steps, [(late_in, 16 * 9), (consts_ready, 2)])

        @block.scalar
        def _(act):
            for s in B_SEMS["act"]:
                act.sem_inc(s, 1)
            af = nc.scalar.activation

            def turn_x(b, _):
                act.wait_ge(x_turned, b + 1)
                nc.scalar.copy(x_t[:], a_turned[:, 1, :]).then_inc(x_t_ready, 1)

            def project(b, r):
                for i in range(4 * r, 4 * r + 4, 2):
                    act.wait_ge(projected, 16 * b + i + 1)
                    if i < 8:
                        last = nc.scalar.mul(q_t[:, i, :], head_bank(i), E ** -0.5)
                    elif i < 12:
                        last = nc.scalar.copy(k_t[:, i - 8, :], head_bank(i))
                    else:
                        last = nc.scalar.copy(v[:, i - 12, :], head_bank(i))
                    last.then_inc(proj_act, 1)

            def exponentials(b, n):
                _, _, w = units_pair(n)
                N = UNITS * b + n
                act.wait_ge(negmax_ready, N + 1)
                need(act, turned, N - 1)
                for h in range(2):
                    last = af(prob[:, n % 2, h, 0:w], a_scores[:, h, 0:w], ACT.Exp, bias=negmax[:, n % 2, h:h + 1],
                              accum_out=rowsum[:, n % 2, h:h + 1])
                last.then_inc(exp_done, 1)

            def turn(b, n):
                _, _, w = units_pair(n)
                N = UNITS * b + n
                act.wait_ge(turned, N + 1)
                need(act, valued, N - 1)
                nc.scalar.copy(prob_t[:, n % 2, 0, 0:w], a_turned[:, 0, 0:w]).then_inc(prob_t_act, 1)

            def value(b, n):
                c, i, _ = units_pair(n)
                if i == NT - 1:
                    act.wait_ge(valued, UNITS * b + n + 1)
                    need(act, out_done, b)
                    nc.scalar.copy(z_t[:, c, :], a_z[:]).then_inc(z_ready, 1)

            def shift(b, l, _):
                act.wait_ge(h_done, 2 * b + l + 2)
                nc.scalar.copy(h_t[:], b_misc[:]).then_inc(h_ready, 1)

            def qkv(b, l, t):
                T = 8 * b + 4 * l + t
                act.wait_ge(qkv_done, T + 2)
                act.wait_ge(r2_ready, T + 1)
                act.wait_ge(sq_ready, T + 1)
                nc.scalar.copy(qk[:].rearrange("p s h e -> p s (h e)"), b_pair[:]).then_inc(qk_ready, 1)
                nc.scalar.copy(vb[:, t, :], b_misc[:]).then_inc(vb_ready, 1)
                act.wait_ge(qk_ready, T + 2)
                act.wait_ge(ssq_ready, T + 1)
                af(sq[:], qk[:], ACT.Square).then_inc(sq_ready, 1)

            def turn_qk(b, l, t):
                act.wait_ge(qk_turned, 8 * b + 4 * l + t + 2)
                nc.scalar.copy(qb_t[:].rearrange("p c n -> p (c n)"), b_pair[:, 0, :]).then_inc(qb_ready, 1)

            def b_exp(b, l, t):
                act.wait_ge(b_negmax_ready, 8 * b + 4 * l + t + 2)
                for s in range(2):
                    for c in range(CB):
                        k = s * CB + c
                        last = af(b_prob[:, s, c, :], b_pair[:, s, c * P:(c + 1) * P], ACT.Exp,
                                  bias=b_negmax[:, k:k + 1], accum_out=b_rowsum[:, k:k + 1])
                last.then_inc(b_exp_done, 1)

            def b_turn(b, l, t):
                act.wait_ge(b_turned, 8 * b + 4 * l + t + 2)
                nc.scalar.copy(b_prob_t[:, 0, :, :].rearrange("p c n -> p (c n)"), b_pair[:, 0, :]).then_inc(b_pt_act, 1)

            def b_value(b, l, t):
                act.wait_ge(b_valued, 8 * b + 4 * l + t + 2)
                nc.scalar.copy(o_t[:].rearrange("p c n -> p (c n)"), b_misc[:]).then_inc(o_ready, 1)

            def turn_f(b, l, _):
                act.wait_ge(f_turned, 2 * b + l + 2)
                af(f_t[:], b_misc[:], ACT.Identity, scale=ln_gb[:, l, 0:1], bias=ln_gb[:, l, 1:2]).then_inc(f_ready, 1)

            def ffn(b, l, m):
                if m % 2 == 0:
                    L, ch = 2 * b + l, m // 2
                    k = MCH[ch]
                    bank = b_misc[:] if m % 3 == 2 else b_pair[:, m % 3, :]
                    act.wait_ge(w1_done, 6 * L + m + 2)
                    act.wait_ge(u_ready, CH * L + ch if ch else CH * L + 1)
                    af(gelu[0:k, ch % 2, :], bank[0:k, :], ACT.Gelu, bias=b1[0:k, l, 1, ch:ch + 1]).then_inc(gelu_done, 1)

            steps = {"a_turn_x": turn_x, "a_project": project, "a_scores": exponentials, "a_turn": turn,
                     "a_value": value, "b_shift": shift, "b_qkv": qkv, "b_turn_qk": turn_qk, "b_scores": b_exp,
                     "b_turn_p": b_turn, "b_value": b_value, "b_turn_f": turn_f, "b_ffn": ffn}
            all_sequences(act, "act", steps, [(late_in, 16 * 9)])

        @block.vector
        def _(dve):
            vec = nc.vector
            for s in B_SEMS["dve"]:
                dve.sem_inc(s, 1)
            vec.memset(kb_t[:, :, 0:WIN], 0.0)
            vec.memset(vb_mid[0:WIN, 0, :], 0.0)
            vec.memset(u_t[E:P, CH - 1, :], 0.0).then_inc(chain_a, 1)
            dve.wait_ge(chain_a, 1)
            vec.memset(u_t[B2ROW:B2ROW + 1, CH - 1, :], 1.0)
            dve.wait_ge(tables_in, 32)
            for l in range(LAYERS):
                for s in range(2):
                    scale = scale_bc[:, l, s, :].unsqueeze(1).broadcast_to([P, NT, E])
                    swapped = scale_bc[:, l, s, :].rearrange("p (h e) -> p h e", h=2)[:, ::-1, :]
                    vec.tensor_tensor(table[:, l, 0, :, s, :], rope[:, 0, :, s, :], scale, ALU.mult)
                    for t in range(NT):
                        last = vec.tensor_tensor(table[:, l, 1, t, s, :].rearrange("p (h e) -> p h e", h=2),
                                                 rope[:, 1, t, s, :].rearrange("p (h e) -> p h e", h=2), swapped, ALU.mult)
            last.then_inc(consts_ready, 2)
            count_a, count_b = [0], [0]

            def link(b, ins):
                count_a[0] += 1
                ins.then_inc(chain_a, 1)
                wait_apart(dve, waited_dve, chain_a, b * CHAIN_A + count_a[0] + 1)

            def link_b(b, ins):
                count_b[0] += 1
                ins.then_inc(chain_b, 1)
                wait_apart(dve, waited_dve, chain_b, b * CHAIN_B + count_b[0] + 1)

            def project(b, r):
                if r == 0:
                    count_a[0] = 0
                for i in range(4 * r + 1, 4 * r + 4, 2):
                    dve.wait_ge(projected, 16 * b + i + 1)
                    if i < 8:
                        last = vec.tensor_scalar(q_t[:, i, :], head_bank(i), E ** -0.5, None, ALU.mult)
                    elif i < 12:
                        last = vec.tensor_copy(k_t[:, i - 8, :], head_bank(i))
                    else:
                        last = vec.tensor_copy(v[:, i - 12, :], head_bank(i))
                    last.then_inc(proj_dve, 1)

            def scores(b, n):
                _, _, w = units_pair(n)
                N = UNITS * b + n
                dve.wait_ge(scored, N + 1)
                vec.tensor_reduce(negmax[:, n % 2, :], a_scores[:, :, 0:w], AX.X, ALU.max, negate=True).then_inc(negmax_ready, 1)

            def inverse(b, n):
                dve.wait_ge(exp_done, UNITS * b + n + 1)
                vec.reciprocal(rowinv[:, n % 2, :], rowsum[:, n % 2, :]).then_inc(rowinv_ready, 1)

            def turn(b, n):
                _, _, w = units_pair(n)
                N = UNITS * b + n
                dve.wait_ge(turned, N + 1)
                need(dve, valued, N - 1)
                vec.tensor_copy(prob_t[:, n % 2, 1, 0:w], a_turned[:, 1, 0:w]).then_inc(prob_t_dve, 1)

            def out_a(b, _):
                dve.wait_ge(out_done, b + 1)
                dve.wait_ge(x_res_ready, b + 1)
                link(b, vec.tensor_tensor(y[:].rearrange("p t d -> p (t d)"), a_turned[:, 0, :],
                                          x_res[:].rearrange("p t d -> p (t d)"), ALU.add))
                for t in range(NT):
                    last = vec.bn_stats(st_a[:, t, :], y[:, t, :])
                link(b, last)
                for t in range(NT):
                    last = vec.bn_aggr(mv_a[:, t, :], st_a[:, t, :])
                last.then_inc(var_a_ready, 1)

            def norm_a(b, _):
                dve.wait_ge(rs_a_ready, b + 1)
                for t in range(NT):
                    last = vec.tensor_scalar(x1[:, t, :], y[:, t, :], mv_a[:, t, 0:1], rs_a[:, t:t + 1],
                                             ALU.subtract, ALU.mult)
                last.then_inc(x1_ready, 1)
                assert count_a[0] == CHAIN_A, count_a

            def rotate(b, l, t):
                T = 8 * b + 4 * l + t
                if l == 0 and t == 0:
                    count_b[0] = 0
                dve.wait_ge(qk_ready, T + 2)
                dve.wait_ge(rot_ready, T + 1)
                for s in range(2):
                    cos = table[:, l, 0, t, s, :].unsqueeze(1).broadcast_to([P, HB, E])
                    last = vec.tensor_tensor(r1[:, s, :, :], qk[:, s, :, :], cos, ALU.mult)
                last.then_inc(r1_ready, 1)
                for s in range(2):
                    sin = table[:, l, 1, t, s, :].rearrange("p (h e) -> p h e", h=2).unsqueeze(1)
                    swapped = qk[:, s, :, :].rearrange("p n (h e) -> p n h e", h=2)[:, :, ::-1, :]
                    last = vec.tensor_tensor(r2[:, s, :, :].rearrange("p n (h e) -> p n h e", h=2), swapped,
                                             sin.broadcast_to([P, HB, 2, E // 2]), ALU.mult)
                last.then_inc(r2_ready, 1)

            def lengths(b, l, t):
                T = 8 * b + 4 * l + t
                dve.wait_ge(r2_ready, T + 2)
                vec.tensor_tensor(r1[:], r1[:], r2[:], ALU.add).then_inc(rsum_ready, 1)
                dve.wait_ge(sq_ready, T + 2)
                dve.wait_ge(floor_ready, T + 1)
                vec.tensor_reduce(ssq[:], sq[:].rearrange("p s h e -> p (s h) e"), AX.X, ALU.add).then_inc(ssq_ready, 1)

            def turn_qk(b, l, t):
                dve.wait_ge(qk_turned, 8 * b + 4 * l + t + 2)
                vec.tensor_copy(kb_t[:, :, WIN + t * P:WIN + (t + 1) * P],
                                b_pair[:, 1, :].rearrange("p (c n) -> p c n", c=CB)).then_inc(kb_ready, 1)

            def b_scores(b, l, t):
                T = 8 * b + 4 * l + t
                dve.wait_ge(b_scored, T + 2)
                vec.tensor_reduce(b_negmax[:], b_pair[:].rearrange("p s (c n) -> p (s c) n", c=CB), AX.X, ALU.max,
                                  negate=True).then_inc(b_negmax_ready, 1)

            def b_inverse(b, l, t):
                dve.wait_ge(b_exp_done, 8 * b + 4 * l + t + 2)
                vec.reciprocal(b_rowinv[:], b_rowsum[:]).then_inc(b_rowinv_ready, 1)

            def b_turn(b, l, t):
                dve.wait_ge(b_turned, 8 * b + 4 * l + t + 2)
                vec.tensor_copy(b_prob_t[:, 1, :, :].rearrange("p c n -> p (c n)"), b_pair[:, 1, :]).then_inc(b_pt_dve, 1)

            def b_wo(b, l, t):
                dve.wait_ge(wo_done, 8 * b + 4 * l + t + 2)
                vec.tensor_tensor(x2[:, t, :], b_pair[:, 0, 0:D], (x1 if l == 0 else x3)[:, t, :], ALU.add).then_inc(x2_ready, 1)

            def stats(b, l, _):
                L = 2 * b + l
                dve.wait_ge(x2_ready, 4 * L + 5)
                dve.wait_ge(shifted, L + 2)
                for t in range(NT):
                    vec.bn_stats(st_b[:, t, 0:6], x2[:, t, 0:E])
                    last = vec.bn_stats(st_b[:, t, 6:12], b_misc[:, t * E:(t + 1) * E])
                link_b(b, last)
                for t in range(NT):
                    last = vec.bn_aggr(mv_b[:, t, :], st_b[:, t, :])
                last.then_inc(var_b_ready, 1)

            def norm(b, l, _):
                dve.wait_ge(rs_b_ready, 3 * b + l + 2)
                for t in range(NT):
                    for src, o in ((x2[:, t, 0:E], 0), (b_misc[:, t * E:(t + 1) * E], E)):
                        last = vec.tensor_scalar(x_hat[:, t, o:o + E], src, mv_b[:, t, 0:1], rs_b[:, t:t + 1],
                                                 ALU.subtract, ALU.mult)
                last.then_inc(x_hat_ready, 1)

            def ffn(b, l, m):
                if m % 2:
                    L, ch = 2 * b + l, m // 2
                    k = MCH[ch]
                    bank = b_misc[:] if m % 3 == 2 else b_pair[:, m % 3, :]
                    dve.wait_ge(w1_done, 6 * L + m + 2)
                    dve.wait_ge(gelu_done, CH * L + ch + 2)
                    vec.scalar_tensor_tensor(out=u_t[0:k, ch, :], in0=bank[0:k, :], scalar=b1[0:k, l, 0, ch:ch + 1],
                                             in1=gelu[0:k, ch % 2, :], op0=ALU.add, op1=ALU.mult).then_inc(u_ready, 1)

            def w2_add(b, l, _):
                L = 2 * b + l
                dve.wait_ge(w2_done, L + 2)
                vec.tensor_tensor(x3[:].rearrange("p t d -> p (t d)"), b_misc[:],
                                  x2[:].rearrange("p t d -> p (t d)"), ALU.add).then_inc(x3_ready, 1)

            def end_stats(b, l, _):
                dve.wait_ge(x3_ready, 2 * b + 3)
                dve.wait_ge(y_stored, 16 * b + 16)
                link_b(b, vec.tensor_tensor(x2[:], x3[:], x1[:], ALU.add))
                for t in range(NT):
                    last = vec.bn_stats(st_b[:, t, 0:6], x2[:, t, :])
                link_b(b, last)
                for t in range(NT):
                    last = vec.bn_aggr(mv_b[:, t, :], st_b[:, t, 0:6])
                last.then_inc(var_b_ready, 1)

            def end(b, l, _):
                dve.wait_ge(rs_b_ready, 3 * b + 2 + 2)
                for t in range(NT):
                    last = vec.tensor_scalar(y_out[:, t, :], x2[:, t, :], mv_b[:, t, 0:1], rs_b[:, t:t + 1],
                                             ALU.subtract, ALU.mult)
                last.then_inc(y_out_ready, 1)
                assert count_b[0] == CHAIN_B, count_b

            steps = {"a_project": project, "a_scores": scores, "a_inverse": inverse, "a_turn": turn, "a_out": out_a,
                     "a_norm": norm_a, "b_stats": stats, "b_end_stats": end_stats, "b_end": end, "b_rotate": rotate, "b_lengths": lengths, "b_inverse": b_inverse,
                     "b_turn_qk": turn_qk, "b_scores": b_scores, "b_turn_p": b_turn, "b_wo": b_wo, "b_norm": norm,
                     "b_ffn": ffn, "b_w2": w2_add}
            all_sequences(dve, "dve", steps, [(late_in, 16 * 9), (consts_ready, 2)])

        @block.gpsimd
        def _(pool):
            for s in B_SEMS["pool"]:
                pool.sem_inc(s, 1)
            nc.gpsimd.memset(minus_half[:], -0.5).then_inc(half_ready, 1)
            pool.wait_ge(early_in, 16 * 8)
            pool.wait_ge(half_ready, 1)

            def turn_x(b, _):
                pool.wait_ge(x_loaded, 16 * (b + 1))
                need(pool, x1_ready, b)
                nc.gpsimd.tensor_tensor(x_res[:], x_in[:], bout[:].unsqueeze(1).broadcast_to([P, NT, D]),
                                        ALU.add).then_inc(x_res_ready, 1)

            def scores(b, n):
                _, _, w = units_pair(n)
                wait_apart(pool, waited_pool, rowinv_ready, UNITS * b + n + 1)
                for h in range(2):
                    pr = prob[:, n % 2, h, 0:w]
                    last = nc.gpsimd.tensor_scalar(pr, pr, rowinv[:, n % 2, h:h + 1], 1.0, ALU.mult, ALU.mult)
                last.then_inc(prob_ready, 1)

            def qkv(b, l, t):
                T = 8 * b + 4 * l + t
                wait_apart(pool, waited_pool, ssq_ready, T + 2)
                nc.gpsimd.tensor_scalar(ssq_floor[:], ssq[:], 1e-24, None, ALU.max).then_inc(floor_ready, 1)
                pool.wait_ge(floor_ready, T + 2)
                nc.gpsimd.tensor_tensor(rnorm[:], ssq_floor[:], minus_half[:], ALU.pow).then_inc(rnorm_ready, 1)
                pool.wait_ge(rsum_ready, T + 2)
                pool.wait_ge(rnorm_ready, T + 2)
                pool.wait_ge(qk_turned, T + 1)
                nc.gpsimd.tensor_tensor(rot[:].rearrange("p s h e -> p (s h) e"), r1[:].rearrange("p s h e -> p (s h) e"),
                                        rnorm[:].unsqueeze(2).broadcast_to([P, 2 * HB, E]), ALU.mult).then_inc(rot_ready, 1)

            def b_scores(b, l, t):
                pool.wait_ge(b_rowinv_ready, 8 * b + 4 * l + t + 2)
                pr = b_prob[:].rearrange("p s c n -> p (s c) n")
                nc.gpsimd.tensor_tensor(pr, pr, b_rowinv[:].unsqueeze(2).broadcast_to([P, HB, P]),
                                        ALU.mult).then_inc(b_prob_ready, 1)

            def out_a(b, _):
                wait_apart(pool, waited_pool, var_a_ready, b + 1)
                nc.gpsimd.tensor_scalar(ve_a[:], mv_a[:, :, 1], EPS, None, ALU.add).then_inc(eps_a_ready, 1)
                pool.wait_ge(eps_a_ready, b + 1)
                nc.gpsimd.tensor_tensor(rs_a[:], ve_a[:], minus_half[:, 0:NT], ALU.pow).then_inc(rs_a_ready, 1)

            def inverse_deviation(b, k, _):
                wait_apart(pool, waited_pool, var_b_ready, 3 * b + k + 2)
                nc.gpsimd.tensor_scalar(ve_b[:], mv_b[:, :, 1], EPS, None, ALU.add).then_inc(eps_b_ready, 1)
                pool.wait_ge(eps_b_ready, 3 * b + k + 2)
                nc.gpsimd.tensor_tensor(rs_b[:], ve_b[:], minus_half[:, 0:NT], ALU.pow).then_inc(rs_b_ready, 1)

            all_sequences(pool, "pool", {"a_deviation": out_a, "b_deviation": inverse_deviation, "a_turn_x": turn_x, "a_inverse": scores,
                                         "b_lengths": qkv, "b_inverse": b_scores})


def constants():
    bf = mybir.dt.np(BF16)
    i = np.arange(P)
    q, k = i[:, None], i[None, :]
    causal = np.where(k > q, MASKED, 0.0)
    qw = (i % WIN)[:, None]
    seen = (k >= qw) & (k <= qw + WIN)
    first = seen & ((k >= WIN) | (q >= WIN))
    band = np.stack([np.where(first, 0.0, MASKED), np.where(seen, 0.0, MASKED)], 1)
    half = np.arange(0, E, 2, dtype=np.float32)
    inv_freq = (np.float32(1.0) / np.float32(10000.0) ** (half / np.float32(E))).astype(np.float32)
    t = np.arange(S, dtype=np.float32)
    freqs = t[:, None] * inv_freq[None, :]
    base = (half + np.float32(0.4 * E)) / np.float32(1.4 * E)
    power = (t - S // 2) / np.float32(WIN // 2)
    scale = (base[None, :] ** power[:, None]).astype(np.float32)
    cos, sin = np.cos(freqs), np.sin(freqs)
    rope = np.zeros((2, S, 2, E), np.float32)
    for s, f in enumerate((scale * np.float32(8.0), np.float32(1.0) / scale)):
        rope[0, :, s, :] = np.concatenate([cos * f, cos * f], 1)
        rope[1, :, s, :] = np.concatenate([-sin * f, sin * f], 1)
    rope = rope.reshape(2, NT, P, 2, E).transpose(2, 0, 1, 3, 4)
    last = np.zeros((P, P))
    last[P - 1, 0] = 1.0
    return {
        "ident": np.eye(P, dtype=np.float32), "ident_b": np.eye(P).astype(bf), "causal": causal.astype(bf),
        "band": band.astype(bf), "shift_m": np.eye(P, k=1, dtype=np.float32), "last_m": last.astype(np.float32),
        "rope": np.ascontiguousarray(rope),
    }


def kernel(**inputs):
    import numpy as _np
    import concourse.bacc as _bacc
    from concourse import mybir as _mybir
    from concourse.bass_utils import run_bass_kernel_spmd as _run

    a = {k: _np.asarray(v) for k, v in inputs.items()}
    c = _np.ascontiguousarray
    arrays = constants()
    x = a["L0_attn_resid"]
    arrays["x"] = c(x)
    arrays["wq"] = c(a["L0_attn_W_Q"].reshape(D, 4, 2, 2, E).transpose(0, 1, 3, 2, 4).reshape(D, CA, P))
    arrays["wk"] = c(a["L0_attn_W_K"].reshape(D, GA // 2, P))
    arrays["wv"] = c(a["L0_attn_W_V"].reshape(D, GA * E))
    arrays["wout"] = c(a["L0_attn_W_out"].reshape(E, 4, 2, 2, D).transpose(2, 0, 1, 3, 4).reshape(P, CA, D))
    arrays["bout"] = c(a["L0_attn_b_out"])
    arrays["scales"] = c(_np.stack([a["L0_ffn_q_scale"], a["L0_ffn_k_scale"]], 1))
    arrays["wqkv"] = c(a["L0_ffn_wqkv"].transpose(1, 0, 2))
    arrays["wo"] = c(a["L0_ffn_wo"].reshape(LAYERS, CB, P, D).transpose(2, 0, 1, 3))
    arrays["w1"] = c(a["L0_ffn_w1"].transpose(1, 0, 2))
    w2 = _np.zeros((LAYERS, CH * P, D), _np.float32)
    w2[:, :HID] = a["L0_ffn_w2"]
    w2[:, 2 * P + B2ROW] = a["L0_ffn_b2"]
    arrays["w2"] = c(w2.reshape(LAYERS, CH, P, D).transpose(2, 0, 1, 3))
    b1 = _np.zeros((LAYERS, 2, CH * P), _np.float32)
    b1[:, :, :HID] = a["L0_ffn_b1"].reshape(LAYERS, 2, HID)
    arrays["b1"] = c(b1.reshape(LAYERS, 2, CH, P).transpose(3, 0, 1, 2))
    arrays["ln_gb"] = c(_np.stack([a["L0_ffn_ln_g"], a["L0_ffn_ln_b"]], 1).transpose(2, 0, 1))

    nc = _bacc.Bacc("TRN2", target_bir_lowering=False, num_devices=1)
    feed, t_in = {}, {}
    for name, arr in arrays.items():
        feed[f"in_{name}"] = arr
        t_in[name] = nc.dram_tensor(f"in_{name}", arr.shape, _mybir.dt.from_np(arr.dtype), kind="ExternalInput").ap()
    out = nc.dram_tensor("out_0", (B, S, D), F32, kind="ExternalOutput").ap()
    program(nc, t_in, out)
    r = _run(nc, [feed], core_ids=[0])
    return r.results[0]["out_0"]
```

```python
from collections import namedtuple
from contextlib import ExitStack

import numpy as np

import concourse.bass as bass
from concourse import mybir
from concourse.alu_op_type import AluOpType as ALU

ACT = mybir.ActivationFunctionType
AX = mybir.AxisListType
F32 = mybir.dt.float32
BF16 = mybir.dt.bfloat16

P = 128
B, S, D = 8, 512, 128
NT = S // P
E = 64
HA, GA = 16, 8
CA = HA // 2
UNITS = CA * NT
PROJECTIONS = CA + GA // 2 + NT
LAYERS, HB = 2, 8
CB = HB // 2
WIN = 64
INNER = HB * E
HID = 341
CH = 3
MCH = [128, 128, HID - 256]
EPS = 1e-5
B2ROW = 96
MASKED = -1e30
CUT = 16


def block_a(sequence, units, depth=2):
    work = []

    def step(engine, name, args, ns, *after):
        work.append((engine, (name, args, sequence), ns, [(e, (n, a, sequence)) for e, n, a in after]))

    n0, n1 = units
    if n0 == 0:
        work.append(("sp", ("a_load", (0,), sequence), 2000, []))
        earlier = [("dve", ("a_out", (0,), sequence - 1))]
        work.append(("pe", ("a_turn_x", (0,), sequence), 450, [("sp", ("a_load", (0,), sequence))] + earlier))
        work.append(("pool", ("a_turn_x", (0,), sequence), 1300, [("sp", ("a_load", (0,), sequence))] + earlier))
        step("act", "a_turn_x", (0,), 480, ("pe", "a_turn_x", (0,)))
        for i in range(PROJECTIONS):
            taker = "dve" if i % 2 else "act"
            step("pe", "a_project", (i,), 860, (taker, "a_project", (i - 4,)) if i > 3 else ("act", "a_turn_x", (0,)))
            step(taker, "a_project", (i,), 540, ("pe", "a_project", (i,)))
    for n in range(n0, n1):
        w, u = P * (n % NT + 1), (n,)
        if n < depth:
            before = [("act", "a_project", (PROJECTIONS - 2,)), ("dve", "a_project", (PROJECTIONS - 1,))]
        else:
            before = [("act", "a_value", (n - depth,))]
        step("pe", "a_scores", u, 3.35 * w + 115, *before)
        step("dve", "a_scores", u, 2.1 * w + 130, ("pe", "a_scores", u))
        step("act", "a_scores", u, 1.67 * w + 500, ("dve", "a_scores", u), ("pe", "a_turn", (n - depth,)))
        step("dve", "a_inverse", u, 0.52 * w + 300, ("act", "a_scores", u))
        step("pool", "a_inverse", u, 0.83 * w + 250, ("act", "a_scores", u))
        step("pe", "a_turn", u, 1.7 * w, ("pool", "a_inverse", u), ("dve", "a_inverse", u))
        step("act", "a_turn", u, 0.83 * w + 60, ("pe", "a_turn", u), ("pe", "a_value", (n - depth,)))
        step("dve", "a_turn", u, 1.04 * w + 70, ("pe", "a_turn", u), ("pe", "a_value", (n - depth,)))
        step("pe", "a_value", u, 260 * (n % NT + 1), ("act", "a_turn", u), ("dve", "a_turn", u))
        step("act", "a_value", u, 160, ("pe", "a_value", u))
    if n1 == UNITS:
        for t in range(NT):
            step("pe", "a_out", (t,), 1750, ("act", "a_value", (UNITS - 1,)))
        step("dve", "a_out", (0,), 2150, ("pe", "a_out", (NT - 1,)))
        step("pool", "a_deviation", (0,), 1250, ("dve", "a_out", (0,)))
        work.append(("dve", ("a_norm", (0,), sequence), 1030, [("pool", ("a_deviation", (0,), sequence)),
                                                              ("dve", ("b_end_stats", (LAYERS, 0), sequence - 1))]))
    return work


def block_b(sequence, layers, depth=1):
    work = []

    def step(engine, name, args, ns, *after):
        work.append((engine, (name, args, sequence), ns, [(a[0], (a[1], a[2], (sequence, *a[3:])[-1])) for a in after]))

    for l in layers:
        k = (l, 0)
        before = ("dve", "b_w2", (l - 1, 0)) if l else ("dve", "b_w2", (LAYERS - 1, 0), sequence - 1)
        step("pe", "b_shift", k, 435, ("dve", "a_norm", (0,)), before)
        step("act", "b_shift", k, 500, ("pe", "b_shift", k))
        step("dve", "b_shift", k, 600, ("pe", "b_shift", k))
        for t in range(NT):
            k, past, banks_past = (l, t), (l, t - depth), (l, t - 2 * depth)
            step("pe", "b_qk", k, 1730, ("act", "b_shift", (l, 0)), ("dve", "b_shift", (l, 0)), ("act", "b_value", banks_past), ("dve", "b_wo", banks_past))
            step("act", "b_qk", k, 950, ("pe", "b_qk", k), ("dve", "b_r2", past), ("act", "b_squares", past))
            step("act", "b_squares", k, 950, ("act", "b_qk", k), ("dve", "b_ssq", past), ("pe", "b_turn_qk", past))
            step("pe", "b_v", k, 870, ("act", "b_qk", k))
            step("act", "b_v", k, 480, ("pe", "b_v", k))
            step("sp", "b_v", k, 2000, ("act", "b_v", k))
            step("dve", "b_r1", k, 1200, ("act", "b_qk", k), ("pool", "b_unit", past), ("dve", "b_unit", past))
            step("dve", "b_ssq", k, 1150, ("act", "b_squares", k), ("pool", "b_lengths", past))
            step("dve", "b_r2", k, 1200, ("act", "b_qk", k), ("dve", "b_rsum", past))
            step("dve", "b_rsum", k, 1150, ("dve", "b_r1", k), ("dve", "b_r2", k))
            step("pool", "b_lengths", k, 3200, ("dve", "b_ssq", k), ("pool", "b_unit", past), ("dve", "b_unit", past))
            for e, ns in (("pool", 1000), ("dve", 600)):
                step(e, "b_unit", k, ns, ("pool", "b_lengths", k), ("dve", "b_rsum", k), ("pe", "b_turn_qk", past))
            step("pe", "b_turn_qk", k, 870, ("pool", "b_unit", k), ("dve", "b_unit", k), ("act", "b_v", k))
            step("act", "b_turn_qk", k, 480, ("pe", "b_turn_qk", k), ("pe", "b_scores", past))
            step("dve", "b_turn_qk", k, 600, ("pe", "b_turn_qk", k))
            step("pe", "b_scores", k, 2560, ("act", "b_turn_qk", k), ("dve", "b_turn_qk", k))
            for s in range(2):
                ks = (l, t, s)
                step("dve", "b_max", ks, 600, ("pe", "b_scores", k), ("act", "b_exp", (*past, s)))
                step("act", "b_exp", ks, 1380, ("dve", "b_max", ks), ("pe", "b_turn_p", (*past, s)))
                step("dve", "b_inverse", ks, 750 if s else 90, ("act", "b_exp", ks), ("pool", "b_inverse", (*past, 0)))
                if s == 0:
                    step("pool", "b_inverse", ks, 1000, ("dve", "b_inverse", ks))
                step("pe", "b_turn_p", ks, 435, ("dve" if s else "pool", "b_inverse", ks))
                step("dve" if s else "act", "b_turn_p", ks, 540, ("pe", "b_turn_p", ks), ("pe", "b_value", past))
            step("pe", "b_value", k, 1250, ("act", "b_turn_p", (l, t, 0)), ("dve", "b_turn_p", (l, t, 1)), ("sp", "b_v", k))
            step("act", "b_value", k, 480, ("pe", "b_value", k), ("pe", "b_wo", past))
            step("pe", "b_wo", k, 870, ("act", "b_value", k))
            step("dve", "b_wo", k, 200, ("pe", "b_wo", k), ("dve", "b_end", (LAYERS, 0), sequence - 1))
        k = (l, 0)
        step("pe", "b_stats", k, 750, ("dve", "b_wo", (l, NT - 1)))
        step("dve", "b_stats", k, 1700, ("pe", "b_stats", k))
        step("pool", "b_deviation", k, 1300, ("dve", "b_stats", k))
        step("dve", "b_norm", k, 1900, ("pool", "b_deviation", k))
        step("pe", "b_turn_f", k, 450, ("dve", "b_norm", k))
        step("act", "b_turn_f", k, 650, ("pe", "b_turn_f", k))
        for m in range(2 * CH):
            step("pe", "b_ffn", (l, m), 860, ("act", "b_turn_f", (l, 0)), *([("act", "b_gelu", (l, 0))] if m > 3 else []))
            if m == CH - 1:
                step("act", "b_gelu", (l, 0), 3 * 600 + 1300, ("pe", "b_ffn", (l, m)))
            if m >= CH:
                step("dve", "b_ffn", (l, m), 640, ("pe", "b_ffn", (l, m)), ("act", "b_gelu", (l, 0)))
        k = (l, 0)
        step("pe", "b_w2", k, 2620, ("dve", "b_ffn", (l, 2 * CH - 1)))
        step("dve", "b_w2", k, 600, ("pe", "b_w2", k))
    if LAYERS - 1 in layers:
        k = (LAYERS, 0)
        step("dve", "b_end_stats", k, 2150, ("dve", "b_w2", (LAYERS - 1, 0)))
        step("pool", "b_deviation", k, 1300, ("dve", "b_end_stats", k))
        step("dve", "b_end", k, 1030, ("pool", "b_deviation", k))
        step("sp", "b_end", k, 60, ("dve", "b_end", k))
    return work


ENGINES = ("pe", "act", "dve", "pool", "sp")


def in_order(work, pull, lead, signal):
    ns, after, latest = {}, {}, {}
    for engine, key, t, deps in work:
        step = (engine, key)
        ns[step], after[step] = t, list(deps)
        if (engine, key[0]) in latest:
            after[step].append(latest[engine, key[0]])
        latest[engine, key[0]] = step
    after = {s: [d for d in deps if d in ns] for s, deps in after.items()}
    behind = {s: [] for s in ns}
    for s, deps in after.items():
        for d in deps:
            behind[d].append(s)
    way, waiting = {}, {s: len(b) for s, b in behind.items()}
    ends = [s for s in ns if not waiting[s]]
    while ends:
        s = ends.pop()
        way[s] = ns[s] + max([way[x] + signal for x in behind[s]], default=0)
        for d in after[s]:
            waiting[d] -= 1
            if not waiting[d]:
                ends.append(d)
    free, done, order = dict.fromkeys(ENGINES, 0.0), {}, {e: [] for e in ENGINES}
    left = {s: len(deps) for s, deps in after.items()}
    ready = [s for s in ns if not left[s]]
    while ready:
        start = lambda s: max([free[s[0]]] + [done[d] + signal for d in after[s]])
        s = min(ready, key=lambda s: start(s) - pull * way[s] - lead * (s[1][0][0] == "a"))
        free[s[0]] = done[s] = start(s) + ns[s]
        order[s[0]].append(s[1])
        ready.remove(s)
        for x in behind[s]:
            left[x] -= 1
            if not left[x]:
                ready.append(x)
    assert len(done) == len(ns)
    return order


FIRST_WEIGHTS, LOOP_WEIGHTS, LAST_WEIGHTS = (0.05, 100, 250), (0.04, 300, 220), (0.03, 500, 250)
FIRST = in_order(block_a(0, (0, UNITS), 4) + block_a(1, (0, CUT)) + block_b(0, [0]), *FIRST_WEIGHTS)
LOOP = in_order(block_a(0, (CUT, UNITS)) + block_a(1, (0, CUT)) + block_b(-1, [1]) + block_b(0, [0]), *LOOP_WEIGHTS)
LAST = in_order(block_a(0, (CUT, UNITS)) + block_b(-1, [1]) + block_b(0, [0, 1], 2), *LAST_WEIGHTS)
CHAIN_A, CHAIN_B = 2, 4



def program(nc, t_in, out):
    ctx = ExitStack()
    with ctx:
        def sb(name, shape, dt=F32):
            return ctx.enter_context(nc.sbuf_tensor(name, shape, dt))

        def ps(name, shape):
            return ctx.enter_context(nc.psum_tensor(name, shape, F32))

        def sem(name):
            return ctx.enter_context(nc.semaphore(name))

        ident, ident_b = sb("ident", [P, P]), sb("ident_b", [P, P], BF16)
        causal = sb("causal", [P, P], BF16)
        band = sb("band", [P, 2, P], BF16)
        shift_m, last_m = sb("shift_m", [P, P]), sb("last_m", [P, P])
        rope = sb("rope", [P, 2, NT, 2, E])
        scale_bc = sb("scale_bc", [P, LAYERS, 2, E])
        table = sb("table", [P, LAYERS, 2, NT, 2, E])
        wq, wk, wv = sb("wq", [P, CA, P]), sb("wk", [P, GA // 2, P]), sb("wv", [P, GA * E])
        wout, bout = sb("wout", [P, CA, D]), sb("bout", [P, D])
        wqkv, wo = sb("wqkv", [P, LAYERS, 3 * INNER]), sb("wo", [P, LAYERS, CB, D])
        w1, w2 = sb("w1", [P, LAYERS, 2 * HID]), sb("w2", [P, LAYERS, CH, D])
        b1 = sb("b1", [P, LAYERS, 2, CH])
        ln_gb = sb("ln_gb", [P, LAYERS, 2])
        x_in, x_res, x_t = sb("x_in", [P, NT, D]), sb("x_res", [P, NT, D]), sb("x_t", [P, S])
        q_t, k_t, v = sb("q_t", [P, CA, S]), sb("k_t", [P, GA // 2, S]), sb("v", [P, NT, GA * E])
        negmax, rowsum, rowinv = sb("negmax", [P, 4, 2]), sb("rowsum", [P, 4, 2]), sb("rowinv", [P, 4, 2])
        prob, prob_t = sb("prob", [P, 2, 2, S]), sb("prob_t", [P, 2, 2, S])
        z_t, y = sb("z_t", [P, CA, S]), sb("y", [P, NT, D])
        st_a, mv_a, ve_a, rs_a = sb("st_a", [P, NT, 6]), sb("mv_a", [P, NT, 2]), sb("ve_a", [P, NT]), sb("rs_a", [P, NT])
        x1 = sb("x1", [P, NT, D])
        h_t = sb("h_t", [P, S])
        qk, sq = sb("qk", [P, 2, HB, E]), sb("sq", [P, 2, HB, E])
        r1, r2 = sb("r1", [P, 2, HB, E]), sb("r2", [P, 2, HB, E])
        ssq, ssq_floor, rnorm = sb("ssq", [P, 2, 2 * HB]), sb("ssq_floor", [P, 2, 2 * HB]), sb("rnorm", [P, 2, 2 * HB])
        minus_half = sb("minus_half", [P, 2 * HB])
        qb_t, kb_t = sb("qb_t", [P, CB, P]), sb("kb_t", [P, CB, WIN + S])
        vb, vb_mid = sb("vb", [P, NT, INNER]), sb("vb_mid", [P, NT, INNER])
        b_negmax, b_rowsum, b_rowinv = sb("b_negmax", [P, 2, HB]), sb("b_rowsum", [P, 2, HB]), sb("b_rowinv", [P, 2, HB])
        b_prob, b_prob_t = sb("b_prob", [P, 2, CB, P]), sb("b_prob_t", [P, 2, CB, P])
        o_t = sb("o_t", [P, CB, P])
        x2, x3 = sb("x2", [P, NT, D]), sb("x3", [P, NT, D])
        st_b, mv_b, ve_b, rs_b = sb("st_b", [P, NT, 12]), sb("mv_b", [P, NT, 2]), sb("ve_b", [P, NT]), sb("rs_b", [P, NT])
        x_hat, f_t = sb("x_hat", [P, NT, D]), sb("f_t", [P, S])
        gelu, u_t = sb("gelu", [P, CH, S]), sb("u_t", [P, CH, S])
        y_out = sb("y_out", [P, NT, D])

        a_bank = ps("a_bank", [P, 2, 2, 512])
        b_qk, b_att = ps("b_qk", [P, 2, 512]), ps("b_att", [P, 2, 512])

        early_in, late_in, tables_in = sem("early_in"), sem("late_in"), sem("tables_in")
        consts_ready = sem("consts_ready")
        x_loaded, x_turned, x_t_ready, x_res_ready = sem("x_loaded"), sem("x_turned"), sem("x_t_ready"), sem("x_res_ready")
        projected, proj_act, proj_dve = sem("projected"), sem("proj_act"), sem("proj_dve")
        scored, negmax_ready, exp_done = sem("scored"), sem("negmax_ready"), sem("exp_done")
        rowinv_ready, prob0_ready, prob1_ready, turned = sem("rowinv_ready"), sem("prob0_ready"), sem("prob1_ready"), sem("turned")
        prob_t_act, prob_t_dve, valued, z_ready = sem("prob_t_act"), sem("prob_t_dve"), sem("valued"), sem("z_ready")
        out_done, chain_a, x1_ready = sem("out_done"), sem("chain_a"), sem("x1_ready")
        var_a_ready, eps_a_ready, rs_a_ready = sem("var_a_ready"), sem("eps_a_ready"), sem("rs_a_ready")
        half_ready = sem("half_ready")
        B_SEMS = {}

        def bsem(name, engine):
            s = sem(name)
            B_SEMS.setdefault(engine, []).append(s)
            return s

        h_done, h_ready, h_moved = bsem("h_done", "pe"), bsem("h_ready", "act"), bsem("h_moved", "dve")
        qk_done, v_done, qk_ready, vb_ready = bsem("qk_done", "pe"), bsem("v_done", "pe"), bsem("qk_ready", "act"), bsem("vb_ready", "act")
        sq_ready, r1_ready, r2_ready = bsem("sq_ready", "act"), bsem("r1_ready", "dve"), bsem("r2_ready", "dve")
        ssq_ready, floor_ready, rnorm_ready = bsem("ssq_ready", "dve"), bsem("floor_ready", "pool"), bsem("rnorm_ready", "pool")
        var_b_ready, eps_b_ready, rs_b_ready = bsem("var_b_ready", "dve"), bsem("eps_b_ready", "pool"), bsem("rs_b_ready", "pool")
        rsum_ready, qk_turned = bsem("rsum_ready", "dve"), bsem("qk_turned", "pe")
        rot_q_ready, rot_k_ready = bsem("rot_q_ready", "pool"), bsem("rot_k_ready", "dve")
        qb_ready, kb_ready = bsem("qb_ready", "act"), bsem("kb_ready", "dve")
        b_scored, b_negmax_ready, b_exp_done = bsem("b_scored", "pe"), bsem("b_negmax_ready", "dve"), bsem("b_exp_done", "act")
        b_rowinv_ready, b_turned = bsem("b_rowinv_ready", "dve"), bsem("b_turned", "pe")
        b_prob0_ready, b_prob1_ready = bsem("b_prob0_ready", "pool"), bsem("b_prob1_ready", "dve")
        b_pt_act, b_pt_dve = bsem("b_pt_act", "act"), bsem("b_pt_dve", "dve")
        b_valued, o_ready, wo_done, x2_ready = bsem("b_valued", "pe"), bsem("o_ready", "act"), bsem("wo_done", "pe"), bsem("x2_ready", "dve")
        shifted, chain_b, x_hat_ready = bsem("shifted", "pe"), bsem("chain_b", "dve"), bsem("x_hat_ready", "dve")
        f_turned, f_ready, w1_done = bsem("f_turned", "pe"), bsem("f_ready", "act"), bsem("w1_done", "pe")
        gelu_done, u_ready, w2_done, x3_ready = bsem("gelu_done", "act"), bsem("u_ready", "dve"), bsem("w2_done", "pe"), bsem("x3_ready", "dve")
        y_out_ready = bsem("y_out_ready", "dve")
        y_stored = sem("y_stored")
        v_hi = [sem(f"v_hi{t}") for t in range(NT)]
        v_lo = [sem(f"v_lo{t}") for t in range(NT)]

        unit_sets = [(a_bank[:, k, :, :], prob[:, k, :, :], prob_t[:, k, :, :]) for k in range(2)]
        unit_sets.append((b_att[:], b_prob[:].rearrange("p s c n -> p s (c n)"), b_prob_t[:].rearrange("p s c n -> p s (c n)")))
        unit_sets.append((b_qk[:], r1[:].rearrange("p s h e -> p s (h e)"), r2[:].rearrange("p s h e -> p s (h e)")))

        def in_flight(b):
            return 4 if type(b) is int and b == 0 else 2

        def unit_set(b, n):
            k = n % in_flight(b)
            return (*unit_sets[k], k)

        def in_heads(ap):
            return ap.rearrange("p s (h e) -> p s h e", h=HB)

        def in_pairs(ap):
            return ap.rearrange("p (c n) -> p c n", c=CB)

        TileSet = namedtuple("TileSet", "qk sq r1 r2 qb_t prob prob_t o_t k")
        tile_sets = [TileSet(qk[:], sq[:], r1[:], r2[:], qb_t[:], b_prob[:], b_prob_t[:], o_t[:], 0),
                     TileSet(in_heads(k_t[:, 0:2, :]), in_heads(k_t[:, 2:4, :]),
                             in_heads(v[:, 0:2, :]), in_heads(v[:, 2:4, :]), in_pairs(q_t[:, 0, :]),
                             prob[:, 0, :, :].rearrange("p s (c n) -> p s c n", c=CB),
                             prob_t[:, 0, :, :].rearrange("p s (c n) -> p s c n", c=CB), in_pairs(q_t[:, 1, :]), 1)]

        def tiles_in_flight(b):
            return 2 if type(b) is int and b == B - 1 else 1

        def tile_set(b, t):
            return tile_sets[t % tiles_in_flight(b)]

        def tile_bank(b, t):
            return (b_att[:], b_qk[:], a_bank[:, 0, :, :], a_bank[:, 1, :, :])[t % (2 * tiles_in_flight(b))]

        def head_bank(i):
            return a_bank[:, i % 4 // 2, i % 2, :]

        def ffn_bank(m):
            return (b_qk if m % 4 >= 2 else b_att)[:, m % 2, :]

        def units_pair(n):
            return n // NT, n % NT, P * (n % NT + 1)

        def walk(order, b, steps):
            for name, args, sequence in order:
                steps[name](b + sequence, *args)

        def all_sequences(eng, engine, steps, between=()):
            order = FIRST[engine]
            k = [name[0] for name, _, _ in order].index("b")
            walk(order[:k], 0, steps)
            for s, value in between:
                eng.wait_ge(s, value)
            walk(order[k:], 0, steps)
            with eng.Fori(1, B - 1) as b:
                walk(LOOP[engine], b, steps)
            walk(LAST[engine], B - 1, steps)

        def need(eng, s, value):
            if not (type(value) is int and value <= 0):
                eng.wait_ge(s, value)

        waited_dve, waited_pool = sem("waited_dve"), sem("waited_pool")

        def wait_apart(eng, passed, s, value):
            eng.wait_ge(s, value)
            eng.sem_inc(passed, 1)

        block = ctx.enter_context(nc.Block())

        @block.sync
        def _(sp):
            for dst, src in ((ident, "ident"), (causal, "causal"), (ident_b, "ident_b"), (wq, "wq"), (wk, "wk"),
                             (wv, "wv"), (wout, "wout")):
                sp.dma_start(dst[:], t_in[src]).then_inc(early_in, 16)
            sp.dma_start(bout[:], t_in["bout"].partition_broadcast(P)).then_inc(early_in, 16)
            sp.sem_inc(y_stored, 16)

            def load(b, _):
                need(sp, x_turned, b)
                need(sp, x_res_ready, b)
                src = t_in["x"][b] if type(b) is int else t_in["x"][bass.ds(b, 1)].rearrange("o s d -> (o s) d")
                sp.dma_start(x_in[:], src.rearrange("(t p) d -> p t d", p=P)).then_inc(x_loaded, 16)

            load(0, 0)
            sp.dma_start(rope[:], t_in["rope"]).then_inc(tables_in, 16)
            sp.dma_start(scale_bc[:], t_in["scales"].partition_broadcast(P)).then_inc(tables_in, 16)
            for dst, src in ((band, "band"), (shift_m, "shift_m"), (last_m, "last_m"), (wqkv, "wqkv"), (wo, "wo"),
                             (w1, "w1"), (w2, "w2"), (b1, "b1"), (ln_gb, "ln_gb")):
                sp.dma_start(dst[:], t_in[src]).then_inc(late_in, 16)

            def v_shift(b, l, t):
                sp.wait_ge(vb_ready, 8 * b + 4 * l + t + 2)
                sp.dma_start(vb_mid[WIN:P, t, :], vb[0:WIN, t, :]).then_inc(v_hi[t], 16)
                if t + 1 < NT:
                    sp.dma_start(vb_mid[0:WIN, t + 1, :], vb[WIN:P, t, :]).then_inc(v_lo[t + 1], 16)

            def store(b, l, _):
                sp.wait_ge(y_out_ready, b + 2)
                if type(b) is int:
                    dst = out[b]
                else:
                    dst = out[bass.ds(b, 1)].rearrange("o s d -> (o s) d")
                sp.dma_start(dst.rearrange("(t p) d -> p t d", p=P), y_out[:]).then_inc(y_stored, 16)

            steps = {"a_load": load, "b_v": v_shift, "b_end": store}
            walk(FIRST["sp"][1:], 0, steps)
            with sp.Fori(1, B - 1) as b:
                walk(LOOP["sp"], b, steps)
            walk(LAST["sp"], B - 1, steps)
            sp.wait_ge(y_stored, 16 * (B + 1))

        @block.tensor
        def _(pe):
            for s in B_SEMS["pe"]:
                pe.sem_inc(s, 1)
            pe.wait_ge(early_in, 16 * 8)
            mm = nc.tensor.matmul

            def turn_x(b, _):
                pe.wait_ge(x_loaded, 16 * (b + 1))
                need(pe, prob_t_dve, UNITS * b)
                need(pe, var_a_ready, b)
                for t in range(NT):
                    last = nc.tensor.transpose(a_bank[:, 1, 1, t * P:(t + 1) * P], x_in[:, t, :], ident[:])
                last.then_inc(x_turned, 1)

            def project(b, i):
                if i == 0:
                    pe.wait_ge(x_t_ready, b + 1)
                    need(pe, z_ready, UNITS * b)
                if i >= 4:
                    pe.wait_ge(proj_dve if i % 2 else proj_act, 8 * b + i // 2 - 1)
                if i < 8:
                    last = mm(head_bank(i), wq[:, i, :], x_t[:], start=True, stop=True)
                elif i < 12:
                    last = mm(head_bank(i), wk[:, i - 8, :], x_t[:], start=True, stop=True)
                else:
                    last = mm(head_bank(i), x_t[:, (i - 12) * P:(i - 11) * P], wv[:], start=True, stop=True)
                last.then_inc(projected, 1)

            def scores(b, n):
                c, i, w = units_pair(n)
                if n == 0:
                    pe.wait_ge(proj_act, 8 * b + 8)
                    pe.wait_ge(proj_dve, 8 * b + 8)
                elif n >= in_flight(b):
                    pe.wait_ge(z_ready, UNITS * b + n + 1 - in_flight(b))
                bank, _, _, _ = unit_set(b, n)
                for h in range(2):
                    half = slice(E * h, E * h + E)
                    mm(bank[:, h, 0:w], q_t[half, c, i * P:(i + 1) * P], k_t[half, c // 2, 0:w],
                       start=True, stop=False)
                for h in range(2):
                    last = mm(bank[:, h, w - P:w], ident_b[:], causal[:], start=False, stop=True)
                last.then_inc(scored, 1)

            def turn(b, n):
                _, i, _ = units_pair(n)
                pe.wait_ge(prob0_ready, UNITS * b + n + 1)
                pe.wait_ge(prob1_ready, UNITS * b + n + 1)
                bank, pr, _, _ = unit_set(b, n)
                for h in range(2):
                    for j in range(i + 1):
                        last = nc.tensor.transpose(bank[:, h, j * P:(j + 1) * P], pr[:, h, j * P:(j + 1) * P], ident[:])
                last.then_inc(turned, 1)

            def value(b, n):
                c, i, _ = units_pair(n)
                pe.wait_ge(prob_t_act, UNITS * b + n + 1)
                pe.wait_ge(prob_t_dve, UNITS * b + n + 1)
                bank, _, pr_t, _ = unit_set(b, n)
                for j in range(i + 1):
                    for h in range(2):
                        g = 2 * (c // 2) + h
                        last = mm(bank[E * h:E * h + E, 0, 0:P], v[:, j, g * E:(g + 1) * E],
                                  pr_t[:, h, j * P:(j + 1) * P], start=(j == 0), stop=(j == i))
                last.then_inc(valued, 1)

            def out_a(b, t):
                if t == 0:
                    pe.wait_ge(z_ready, UNITS * b + UNITS)
                for c in range(CA):
                    last = mm(a_bank[:, 0, 0, t * P:(t + 1) * P], z_t[:, c, t * P:(t + 1) * P], wout[:, c, :],
                              start=(c == 0), stop=(c == CA - 1))
                if t == NT - 1:
                    last.then_inc(out_done, 1)

            def shift(b, l, _):
                src = x1 if l == 0 else x3
                if l == 0:
                    pe.wait_ge(x1_ready, b + 1)
                pe.wait_ge(x3_ready, 2 * b + l + 1)
                for t in range(NT):
                    last = nc.tensor.transpose(b_att[:, 1, t * P:(t + 1) * P], src[:, t, :], ident[:])
                last.then_inc(h_done, 1)

            def qkv(b, l, t):
                bank = tile_bank(b, t)
                T = 8 * b + 4 * l + t
                if t == 0:
                    pe.wait_ge(h_ready, 2 * b + l + 2)
                    pe.wait_ge(h_moved, 2 * b + l + 2)
                    pe.wait_ge(u_ready, CH * (2 * b + l) + 1)
                elif t >= 2 * tiles_in_flight(b):
                    pe.wait_ge(o_ready, T)
                    pe.wait_ge(x2_ready, T)
                lhs = h_t[:, t * P:(t + 1) * P]
                mm(bank[:, 0, :], lhs, wqkv[:, l, 0:INNER], start=True, stop=True)
                mm(bank[:, 1, :], lhs, wqkv[:, l, INNER:2 * INNER], start=True, stop=True).then_inc(qk_done, 1)

            def value_in(b, l, t):
                bank = tile_bank(b, t)
                pe.wait_ge(qk_ready, 8 * b + 4 * l + t + 2)
                mm(bank[:, 0, :], h_t[:, t * P:(t + 1) * P], wqkv[:, l, 2 * INNER:], start=True, stop=True).then_inc(v_done, 1)

            def turn_qk(b, l, t):
                u = tile_set(b, t)
                bank = tile_bank(b, t)
                T = 8 * b + 4 * l + t
                pe.wait_ge(rot_q_ready, T + 2)
                pe.wait_ge(rot_k_ready, T + 2)
                pe.wait_ge(vb_ready, T + 2)
                for s in range(2):
                    for c in range(CB):
                        last = nc.tensor.transpose(bank[:, s, c * P:(c + 1) * P],
                                                   u.sq[:, s, 2 * c:2 * c + 2, :].rearrange("p h e -> p (h e)"), ident[:])
                last.then_inc(qk_turned, 1)

            def b_score(b, l, t):
                u = tile_set(b, t)
                bank = tile_bank(b, t)
                T = 8 * b + 4 * l + t
                pe.wait_ge(qb_ready, T + 2)
                pe.wait_ge(kb_ready, T + 2)
                for s in range(2):
                    mm(bank[:, s, :], ident_b[:],
                       band[:, min(t, 1), :].unsqueeze(1).broadcast_to([P, CB, P]), start=True, stop=True)
                for c in range(CB):
                    for w in range(2):
                        for s in range(2):
                            half = slice(E * s, E * s + E)
                            k0 = t * P + WIN * w
                            last = mm(bank[WIN * w:WIN * w + WIN, s, c * P:(c + 1) * P],
                                      u.qb_t[half, c, WIN * w:WIN * w + WIN], kb_t[half, c, k0:k0 + P],
                                      start=False, stop=True, skip_group_check=True)
                last.then_inc(b_scored, 1)

            def b_turn(b, l, t, s):
                u = tile_set(b, t)
                bank = tile_bank(b, t)
                pe.wait_ge(b_prob1_ready if s else b_prob0_ready, 8 * b + 4 * l + t + 2)
                for c in range(CB):
                    last = nc.tensor.transpose(bank[:, s, c * P:(c + 1) * P], u.prob[:, s, c, :], ident[:])
                last.then_inc(b_turned, 1)

            def b_value(b, l, t):
                u = tile_set(b, t)
                bank = tile_bank(b, t)
                T = 8 * b + 4 * l + t
                pe.wait_ge(b_pt_act, T + 2)
                pe.wait_ge(b_pt_dve, T + 2)
                pe.wait_ge(v_hi[t], 16 * (2 * b + l) + 16)
                if t:
                    pe.wait_ge(v_lo[t], 16 * (2 * b + l) + 16)
                pe.wait_ge(vb_ready, T + 2)
                for c in range(CB):
                    for w in range(2):
                        for s in range(2):
                            h = 2 * c + s
                            src = vb if w else vb_mid
                            last = mm(bank[E * s:E * s + E, 0, c * P + WIN * w:c * P + WIN * w + WIN],
                                      src[:, t, h * E:(h + 1) * E], u.prob_t[:, s, c, WIN * w:WIN * w + WIN],
                                      start=True, stop=True)
                last.then_inc(b_valued, 1)

            def b_wo(b, l, t):
                u = tile_set(b, t)
                bank = tile_bank(b, t)
                pe.wait_ge(o_ready, 8 * b + 4 * l + t + 2)
                for c in range(CB):
                    last = mm(bank[:, 1, 0:D], u.o_t[:, c, :], wo[:, l, c, :], start=(c == 0), stop=(c == CB - 1))
                last.then_inc(wo_done, 1)

            def norm(b, l, _):
                pe.wait_ge(x2_ready, 8 * b + 4 * l + 5)
                mm(b_qk[:, 0, 0:NT * E], shift_m[:], x2[:, :, E:P], start=True, stop=True)
                last = mm(b_qk[:, 0, E:NT * E], last_m[:], x2[:, 0:NT - 1, E:P], start=False, stop=True,
                          skip_group_check=True)
                last.then_inc(shifted, 1)

            def turn_f(b, l, _):
                pe.wait_ge(x_hat_ready, 2 * b + l + 2)
                for t in range(NT):
                    last = nc.tensor.transpose(b_qk[:, 1, t * P:(t + 1) * P], x_hat[:, t, :], ident[:])
                last.then_inc(f_turned, 1)

            def ffn(b, l, m):
                L = 2 * b + l
                ch, part = m % CH, 1 - m // CH
                if m == 0:
                    pe.wait_ge(f_ready, L + 2)
                if m > 3:
                    pe.wait_ge(gelu_done, CH * L + m - 2)
                o = part * HID + ch * P
                mm(ffn_bank(m)[0:MCH[ch], :], w1[:, l, o:o + MCH[ch]], f_t[:], start=True, stop=True).then_inc(w1_done, 1)

            def w2_mul(b, l, _):
                L = 2 * b + l
                pe.wait_ge(u_ready, CH * L + CH + 1)
                for t in range(NT):
                    for ch in range(CH):
                        last = mm(b_att[:, 0, t * P:(t + 1) * P], u_t[:, ch, t * P:(t + 1) * P], w2[:, l, ch, :],
                                  start=(ch == 0), stop=(ch == CH - 1))
                last.then_inc(w2_done, 1)

            steps = {"a_turn_x": turn_x, "a_project": project, "a_scores": scores, "a_turn": turn, "a_value": value,
                     "a_out": out_a, "b_shift": shift, "b_qk": qkv, "b_v": value_in, "b_turn_qk": turn_qk, "b_scores": b_score,
                     "b_turn_p": b_turn, "b_value": b_value, "b_wo": b_wo, "b_stats": norm, "b_turn_f": turn_f,
                     "b_ffn": ffn, "b_w2": w2_mul}
            all_sequences(pe, "pe", steps, [(late_in, 16 * 9), (consts_ready, 2)])

        @block.scalar
        def _(act):
            for s in B_SEMS["act"]:
                act.sem_inc(s, 1)
            af = nc.scalar.activation

            def turn_x(b, _):
                act.wait_ge(x_turned, b + 1)
                nc.scalar.copy(x_t[:], a_bank[:, 1, 1, :]).then_inc(x_t_ready, 1)

            def project(b, i):
                act.wait_ge(projected, 16 * b + i + 1)
                if i < 8:
                    last = nc.scalar.mul(q_t[:, i, :], head_bank(i), E ** -0.5)
                elif i < 12:
                    last = nc.scalar.copy(k_t[:, i - 8, :], head_bank(i))
                else:
                    last = nc.scalar.copy(v[:, i - 12, :], head_bank(i))
                last.then_inc(proj_act, 1)

            def exponentials(b, n):
                _, _, w = units_pair(n)
                N = UNITS * b + n
                need(act, turned, N + 1 - in_flight(b))
                bank, pr, _, k = unit_set(b, n)
                for h in range(2):
                    act.wait_ge(negmax_ready, 2 * N + h + 1)
                    af(pr[:, h, 0:w], bank[:, h, 0:w], ACT.Exp, bias=negmax[:, k, h:h + 1], accum_out=rowsum[:, k, h:h + 1]).then_inc(exp_done, 1)

            def turn(b, n):
                _, _, w = units_pair(n)
                N = UNITS * b + n
                act.wait_ge(turned, N + 1)
                need(act, valued, N + 1 - in_flight(b))
                bank, _, pr_t, _ = unit_set(b, n)
                nc.scalar.copy(pr_t[:, 0, 0:w], bank[:, 0, 0:w]).then_inc(prob_t_act, 1)

            def value(b, n):
                c, i, _ = units_pair(n)
                act.wait_ge(valued, UNITS * b + n + 1)
                need(act, out_done, b)
                bank, _, _, _ = unit_set(b, n)
                nc.scalar.copy(z_t[:, c, i * P:(i + 1) * P], bank[:, 0, 0:P]).then_inc(z_ready, 1)

            def shift(b, l, _):
                act.wait_ge(h_done, 2 * b + l + 2)
                nc.scalar.copy(h_t[0:E, :], b_att[0:E, 1, :]).then_inc(h_ready, 1)

            def qkv(b, l, t):
                u = tile_set(b, t)
                bank = tile_bank(b, t)
                T = 8 * b + 4 * l + t
                act.wait_ge(qk_done, T + 2)
                act.wait_ge(r2_ready, T + 2 - tiles_in_flight(b))
                act.wait_ge(sq_ready, T + 2 - tiles_in_flight(b))
                nc.scalar.copy(u.qk[:].rearrange("p s h e -> p s (h e)"), bank[:]).then_inc(qk_ready, 1)

            def squares(b, l, t):
                u = tile_set(b, t)
                T = 8 * b + 4 * l + t
                act.wait_ge(qk_ready, T + 2)
                act.wait_ge(qk_turned, T + 2 - tiles_in_flight(b))
                act.wait_ge(ssq_ready, T + 2 - tiles_in_flight(b))
                af(u.sq[:], u.qk[:], ACT.Square).then_inc(sq_ready, 1)

            def value_out(b, l, t):
                bank = tile_bank(b, t)
                act.wait_ge(v_done, 8 * b + 4 * l + t + 2)
                nc.scalar.copy(vb[:, t, :], bank[:, 0, :]).then_inc(vb_ready, 1)

            def turn_qk(b, l, t):
                u = tile_set(b, t)
                bank = tile_bank(b, t)
                act.wait_ge(qk_turned, 8 * b + 4 * l + t + 2)
                act.wait_ge(b_scored, 8 * b + 4 * l + t + 2 - tiles_in_flight(b))
                nc.scalar.copy(u.qb_t[:].rearrange("p c n -> p (c n)"), bank[:, 0, :]).then_inc(qb_ready, 1)

            def b_exp(b, l, t, s):
                u = tile_set(b, t)
                bank = tile_bank(b, t)
                T = 8 * b + 4 * l + t
                act.wait_ge(b_negmax_ready, 2 * T + s + 2)
                before = 2 * (T - tiles_in_flight(b)) + s + 2
                need(act, b_turned, before)
                need(act, b_rowinv_ready, before)
                for c in range(CB):
                    k = s * CB + c
                    last = af(u.prob[:, s, c, :], bank[:, s, c * P:(c + 1) * P], ACT.Exp,
                              bias=b_negmax[:, u.k, k:k + 1], accum_out=b_rowsum[:, u.k, k:k + 1])
                last.then_inc(b_exp_done, 1)

            def b_turn(b, l, t, _):
                u = tile_set(b, t)
                bank = tile_bank(b, t)
                T = 8 * b + 4 * l + t
                act.wait_ge(b_turned, 2 * T + 2)
                act.wait_ge(b_valued, T + 2 - tiles_in_flight(b))
                nc.scalar.copy(u.prob_t[:, 0, :, :].rearrange("p c n -> p (c n)"), bank[:, 0, :]).then_inc(b_pt_act, 1)

            def b_value(b, l, t):
                u = tile_set(b, t)
                bank = tile_bank(b, t)
                act.wait_ge(b_valued, 8 * b + 4 * l + t + 2)
                act.wait_ge(wo_done, 8 * b + 4 * l + t + 2 - tiles_in_flight(b))
                nc.scalar.copy(u.o_t[:].rearrange("p c n -> p (c n)"), bank[:, 0, :]).then_inc(o_ready, 1)

            def turn_f(b, l, _):
                act.wait_ge(f_turned, 2 * b + l + 2)
                af(f_t[:], b_qk[:, 1, :], ACT.Identity, scale=ln_gb[:, l, 0:1], bias=ln_gb[:, l, 1:2]).then_inc(f_ready, 1)

            def gelus(b, l, _):
                L = 2 * b + l
                act.wait_ge(u_ready, CH * L + 1)
                for ch in range(CH):
                    k = MCH[ch]
                    act.wait_ge(w1_done, 6 * L + ch + 2)
                    af(gelu[0:k, ch, :], ffn_bank(ch)[0:k, :], ACT.Gelu, bias=b1[0:k, l, 1, ch:ch + 1]).then_inc(gelu_done, 1)

            steps = {"a_turn_x": turn_x, "a_project": project, "a_scores": exponentials, "a_turn": turn,
                     "a_value": value, "b_shift": shift, "b_qk": qkv, "b_squares": squares, "b_v": value_out, "b_turn_qk": turn_qk, "b_exp": b_exp,
                     "b_turn_p": b_turn, "b_value": b_value, "b_turn_f": turn_f, "b_gelu": gelus}
            all_sequences(act, "act", steps, [(late_in, 16 * 9)])

        @block.vector
        def _(dve):
            vec = nc.vector
            for s in B_SEMS["dve"]:
                dve.sem_inc(s, 1)
            vec.memset(kb_t[:, :, 0:WIN], 0.0)
            vec.memset(h_t[E:P, 0:1], 0.0)
            vec.memset(vb_mid[0:WIN, 0, :], 0.0)
            vec.memset(u_t[E:P, CH - 1, :], 0.0).then_inc(chain_a, 1)
            dve.wait_ge(chain_a, 1)
            vec.memset(u_t[B2ROW:B2ROW + 1, CH - 1, :], 1.0)
            dve.wait_ge(tables_in, 32)
            for l in range(LAYERS):
                for s in range(2):
                    scale = scale_bc[:, l, s, :].unsqueeze(1).broadcast_to([P, NT, E])
                    swapped = scale_bc[:, l, s, :].rearrange("p (h e) -> p h e", h=2)[:, ::-1, :]
                    vec.tensor_tensor(table[:, l, 0, :, s, :], rope[:, 0, :, s, :], scale, ALU.mult)
                    for t in range(NT):
                        last = vec.tensor_tensor(table[:, l, 1, t, s, :].rearrange("p (h e) -> p h e", h=2),
                                                 rope[:, 1, t, s, :].rearrange("p (h e) -> p h e", h=2), swapped, ALU.mult)
            last.then_inc(consts_ready, 2)
            def link(b, k, ins):
                ins.then_inc(chain_a, 1)
                wait_apart(dve, waited_dve, chain_a, b * CHAIN_A + k + 2)

            def link_b(b, k, ins):
                ins.then_inc(chain_b, 1)
                wait_apart(dve, waited_dve, chain_b, b * CHAIN_B + k + 2)

            def project(b, i):
                dve.wait_ge(projected, 16 * b + i + 1)
                if i < 8:
                    last = vec.tensor_scalar(q_t[:, i, :], head_bank(i), E ** -0.5, None, ALU.mult)
                elif i < 12:
                    last = vec.tensor_copy(k_t[:, i - 8, :], head_bank(i))
                else:
                    last = vec.tensor_copy(v[:, i - 12, :], head_bank(i))
                last.then_inc(proj_dve, 1)

            def scores(b, n):
                _, _, w = units_pair(n)
                N = UNITS * b + n
                dve.wait_ge(scored, N + 1)
                bank, _, _, k = unit_set(b, n)
                for h in range(2):
                    vec.tensor_reduce(negmax[:, k, h:h + 1], bank[:, h, 0:w], AX.X, ALU.max,
                                      negate=True).then_inc(negmax_ready, 1)

            def inverse(b, n):
                _, _, w = units_pair(n)
                N = UNITS * b + n
                _, pr, _, k = unit_set(b, n)
                for h in range(2):
                    dve.wait_ge(exp_done, 2 * N + h + 1)
                    vec.reciprocal(rowinv[:, k, h:h + 1], rowsum[:, k, h:h + 1]).then_inc(rowinv_ready, 1)
                wait_apart(dve, waited_dve, rowinv_ready, 2 * N + 2)
                vec.tensor_scalar(pr[:, 1, 0:w], pr[:, 1, 0:w], rowinv[:, k, 1:2], 1.0,
                                  ALU.mult, ALU.mult).then_inc(prob1_ready, 1)

            def turn(b, n):
                _, _, w = units_pair(n)
                N = UNITS * b + n
                dve.wait_ge(turned, N + 1)
                need(dve, valued, N + 1 - in_flight(b))
                bank, _, pr_t, _ = unit_set(b, n)
                vec.tensor_copy(pr_t[:, 1, 0:w], bank[:, 1, 0:w]).then_inc(prob_t_dve, 1)

            def out_a(b, _):
                dve.wait_ge(out_done, b + 1)
                dve.wait_ge(x_res_ready, b + 1)
                link(b, 0, vec.tensor_tensor(y[:].rearrange("p t d -> p (t d)"), a_bank[:, 0, 0, :],
                                          x_res[:].rearrange("p t d -> p (t d)"), ALU.add))
                for t in range(NT):
                    last = vec.bn_stats(st_a[:, t, :], y[:, t, :])
                link(b, 1, last)
                for t in range(NT):
                    last = vec.bn_aggr(mv_a[:, t, :], st_a[:, t, :])
                last.then_inc(var_a_ready, 1)

            def norm_a(b, _):
                dve.wait_ge(rs_a_ready, b + 1)
                for t in range(NT):
                    last = vec.tensor_scalar(x1[:, t, :], y[:, t, :], mv_a[:, t, 0:1], rs_a[:, t:t + 1],
                                             ALU.subtract, ALU.mult)
                last.then_inc(x1_ready, 1)

            def shift(b, l, _):
                dve.wait_ge(h_done, 2 * b + l + 2)
                vec.tensor_copy(h_t[E:P, 1:S], b_att[E:P, 1, 0:S - 1]).then_inc(h_moved, 1)

            def cosines(b, l, t):
                u = tile_set(b, t)
                T = 8 * b + 4 * l + t
                dve.wait_ge(qk_ready, T + 2)
                dve.wait_ge(rot_q_ready, T + 2 - tiles_in_flight(b))
                dve.wait_ge(rot_k_ready, T + 2 - tiles_in_flight(b))
                for s in range(2):
                    cos = table[:, l, 0, t, s, :].unsqueeze(1).broadcast_to([P, HB, E])
                    last = vec.tensor_tensor(u.r1[:, s, :, :], u.qk[:, s, :, :], cos, ALU.mult)
                last.then_inc(r1_ready, 1)

            def sines(b, l, t):
                u = tile_set(b, t)
                T = 8 * b + 4 * l + t
                dve.wait_ge(qk_ready, T + 2)
                dve.wait_ge(rsum_ready, T + 2 - tiles_in_flight(b))
                for s in range(2):
                    sin = table[:, l, 1, t, s, :].rearrange("p (h e) -> p h e", h=2).unsqueeze(1)
                    swapped = u.qk[:, s, :, :].rearrange("p n (h e) -> p n h e", h=2)[:, :, ::-1, :]
                    last = vec.tensor_tensor(u.r2[:, s, :, :].rearrange("p n (h e) -> p n h e", h=2), swapped,
                                             sin.broadcast_to([P, HB, 2, E // 2]), ALU.mult)
                last.then_inc(r2_ready, 1)

            def rotated(b, l, t):
                u = tile_set(b, t)
                T = 8 * b + 4 * l + t
                dve.wait_ge(r1_ready, T + 2)
                dve.wait_ge(r2_ready, T + 2)
                vec.tensor_tensor(u.r1[:], u.r1[:], u.r2[:], ALU.add).then_inc(rsum_ready, 1)

            def unit_k(b, l, t):
                u = tile_set(b, t)
                T = 8 * b + 4 * l + t
                dve.wait_ge(rsum_ready, T + 2)
                dve.wait_ge(rnorm_ready, T + 2)
                dve.wait_ge(qk_turned, T + 2 - tiles_in_flight(b))
                vec.tensor_tensor(u.sq[:, 1, :, :], u.r1[:, 1, :, :], rnorm[:, u.k, HB:].unsqueeze(2).broadcast_to([P, HB, E]),
                                  ALU.mult).then_inc(rot_k_ready, 1)

            def square_sums(b, l, t):
                u = tile_set(b, t)
                T = 8 * b + 4 * l + t
                dve.wait_ge(sq_ready, T + 2)
                dve.wait_ge(floor_ready, T + 2 - tiles_in_flight(b))
                vec.tensor_reduce(ssq[:, u.k, :], u.sq[:].rearrange("p s h e -> p (s h) e"), AX.X, ALU.add).then_inc(ssq_ready, 1)

            def turn_qk(b, l, t):
                bank = tile_bank(b, t)
                dve.wait_ge(qk_turned, 8 * b + 4 * l + t + 2)
                vec.tensor_copy(kb_t[:, :, WIN + t * P:WIN + (t + 1) * P],
                                bank[:, 1, :].rearrange("p (c n) -> p c n", c=CB)).then_inc(kb_ready, 1)

            def b_max(b, l, t, s):
                u = tile_set(b, t)
                bank = tile_bank(b, t)
                T = 8 * b + 4 * l + t
                dve.wait_ge(b_scored, T + 2)
                need(dve, b_exp_done, 2 * (T - tiles_in_flight(b)) + s + 2)
                vec.tensor_reduce(b_negmax[:, u.k, s * CB:(s + 1) * CB], bank[:, s, :].rearrange("p (c n) -> p c n", c=CB),
                                  AX.X, ALU.max, negate=True).then_inc(b_negmax_ready, 1)

            def b_inverse(b, l, t, s):
                u = tile_set(b, t)
                k = 2 * (8 * b + 4 * l + t) + s + 2
                dve.wait_ge(b_exp_done, k)
                if s == 0:
                    dve.wait_ge(b_prob0_ready, 8 * b + 4 * l + t + 2 - tiles_in_flight(b))
                pairs = slice(s * CB, (s + 1) * CB)
                vec.reciprocal(b_rowinv[:, u.k, pairs], b_rowsum[:, u.k, pairs]).then_inc(b_rowinv_ready, 1)
                if s:
                    dve.wait_ge(b_rowinv_ready, k)
                    vec.tensor_tensor(u.prob[:, 1, :, :], u.prob[:, 1, :, :], b_rowinv[:, u.k, pairs].unsqueeze(2).broadcast_to([P, CB, P]),
                                      ALU.mult).then_inc(b_prob1_ready, 1)

            def b_turn(b, l, t, _):
                u = tile_set(b, t)
                bank = tile_bank(b, t)
                T = 8 * b + 4 * l + t
                dve.wait_ge(b_turned, 2 * T + 3)
                dve.wait_ge(b_valued, T + 2 - tiles_in_flight(b))
                vec.tensor_copy(u.prob_t[:, 1, :, :].rearrange("p c n -> p (c n)"), bank[:, 1, :]).then_inc(b_pt_dve, 1)

            def b_wo(b, l, t):
                bank = tile_bank(b, t)
                dve.wait_ge(wo_done, 8 * b + 4 * l + t + 2)
                vec.tensor_tensor(x2[:, t, :], bank[:, 1, 0:D], (x1 if l == 0 else x3)[:, t, :], ALU.add).then_inc(x2_ready, 1)

            def stats(b, l, _):
                L = 2 * b + l
                dve.wait_ge(x2_ready, 4 * L + 5)
                dve.wait_ge(shifted, L + 2)
                for t in range(NT):
                    vec.bn_stats(st_b[:, t, 0:6], x2[:, t, 0:E])
                    last = vec.bn_stats(st_b[:, t, 6:12], b_qk[:, 0, t * E:(t + 1) * E])
                link_b(b, l, last)
                for t in range(NT):
                    last = vec.bn_aggr(mv_b[:, t, :], st_b[:, t, :])
                last.then_inc(var_b_ready, 1)

            def norm(b, l, _):
                dve.wait_ge(rs_b_ready, 3 * b + l + 2)
                for t in range(NT):
                    for src, o in ((x2[:, t, 0:E], 0), (b_qk[:, 0, t * E:(t + 1) * E], E)):
                        last = vec.tensor_scalar(x_hat[:, t, o:o + E], src, mv_b[:, t, 0:1], rs_b[:, t:t + 1],
                                                 ALU.subtract, ALU.mult)
                last.then_inc(x_hat_ready, 1)

            def ffn(b, l, m):
                L, ch = 2 * b + l, m - CH
                k = MCH[ch]
                dve.wait_ge(w1_done, 6 * L + m + 2)
                dve.wait_ge(gelu_done, CH * L + ch + 2)
                vec.scalar_tensor_tensor(out=u_t[0:k, ch, :], in0=ffn_bank(m)[0:k, :], scalar=b1[0:k, l, 0, ch:ch + 1],
                                         in1=gelu[0:k, ch, :], op0=ALU.add, op1=ALU.mult).then_inc(u_ready, 1)

            def w2_add(b, l, _):
                L = 2 * b + l
                dve.wait_ge(w2_done, L + 2)
                vec.tensor_tensor(x3[:].rearrange("p t d -> p (t d)"), b_att[:, 0, :],
                                  x2[:].rearrange("p t d -> p (t d)"), ALU.add).then_inc(x3_ready, 1)

            def end_stats(b, l, _):
                dve.wait_ge(x3_ready, 2 * b + 3)
                dve.wait_ge(y_stored, 16 * b + 16)
                link_b(b, 2, vec.tensor_tensor(x2[:], x3[:], x1[:], ALU.add))
                for t in range(NT):
                    last = vec.bn_stats(st_b[:, t, 0:6], x2[:, t, :])
                link_b(b, 3, last)
                for t in range(NT):
                    last = vec.bn_aggr(mv_b[:, t, :], st_b[:, t, 0:6])
                last.then_inc(var_b_ready, 1)

            def end(b, l, _):
                dve.wait_ge(rs_b_ready, 3 * b + 2 + 2)
                for t in range(NT):
                    last = vec.tensor_scalar(y_out[:, t, :], x2[:, t, :], mv_b[:, t, 0:1], rs_b[:, t:t + 1],
                                             ALU.subtract, ALU.mult)
                last.then_inc(y_out_ready, 1)

            steps = {"a_project": project, "a_scores": scores, "a_inverse": inverse, "a_turn": turn, "a_out": out_a,
                     "a_norm": norm_a, "b_stats": stats, "b_end_stats": end_stats, "b_end": end, "b_r1": cosines, "b_r2": sines, "b_rsum": rotated, "b_ssq": square_sums, "b_inverse": b_inverse,
                     "b_shift": shift, "b_unit": unit_k, "b_max": b_max, "b_turn_qk": turn_qk, "b_turn_p": b_turn, "b_wo": b_wo, "b_norm": norm,
                     "b_ffn": ffn, "b_w2": w2_add}
            all_sequences(dve, "dve", steps, [(late_in, 16 * 9), (consts_ready, 2)])

        @block.gpsimd
        def _(pool):
            for s in B_SEMS["pool"]:
                pool.sem_inc(s, 1)
            nc.gpsimd.memset(minus_half[:], -0.5).then_inc(half_ready, 1)
            pool.wait_ge(early_in, 16 * 8)
            pool.wait_ge(half_ready, 1)

            def turn_x(b, _):
                pool.wait_ge(x_loaded, 16 * (b + 1))
                need(pool, var_a_ready, b)
                nc.gpsimd.tensor_tensor(x_res[:], x_in[:], bout[:].unsqueeze(1).broadcast_to([P, NT, D]),
                                        ALU.add).then_inc(x_res_ready, 1)

            def scaled(b, n):
                _, _, w = units_pair(n)
                wait_apart(pool, waited_pool, rowinv_ready, 2 * (UNITS * b + n) + 1)
                _, pr, _, k = unit_set(b, n)
                nc.gpsimd.tensor_scalar(pr[:, 0, 0:w], pr[:, 0, 0:w], rowinv[:, k, 0:1], 1.0,
                                        ALU.mult, ALU.mult).then_inc(prob0_ready, 1)

            def lengths(b, l, t):
                u = tile_set(b, t)
                T = 8 * b + 4 * l + t
                wait_apart(pool, waited_pool, ssq_ready, T + 2)
                nc.gpsimd.tensor_scalar(ssq_floor[:, u.k, :], ssq[:, u.k, :], 1e-24, None, ALU.max).then_inc(floor_ready, 1)
                pool.wait_ge(floor_ready, T + 2)
                pool.wait_ge(rot_q_ready, T + 2 - tiles_in_flight(b))
                pool.wait_ge(rot_k_ready, T + 2 - tiles_in_flight(b))
                nc.gpsimd.tensor_tensor(rnorm[:, u.k, :], ssq_floor[:, u.k, :], minus_half[:], ALU.pow).then_inc(rnorm_ready, 1)

            def unit(b, l, t):
                u = tile_set(b, t)
                T = 8 * b + 4 * l + t
                pool.wait_ge(rsum_ready, T + 2)
                pool.wait_ge(rnorm_ready, T + 2)
                pool.wait_ge(qk_turned, T + 2 - tiles_in_flight(b))
                nc.gpsimd.tensor_tensor(u.sq[:, 0, :, :], u.r1[:, 0, :, :], rnorm[:, u.k, 0:HB].unsqueeze(2).broadcast_to([P, HB, E]),
                                        ALU.mult).then_inc(rot_q_ready, 1)

            def b_inverse(b, l, t, _):
                u = tile_set(b, t)
                pool.wait_ge(b_rowinv_ready, 2 * (8 * b + 4 * l + t) + 2)
                nc.gpsimd.tensor_tensor(u.prob[:, 0, :, :], u.prob[:, 0, :, :], b_rowinv[:, u.k, 0:CB].unsqueeze(2).broadcast_to([P, CB, P]),
                                        ALU.mult).then_inc(b_prob0_ready, 1)

            def out_a(b, _):
                wait_apart(pool, waited_pool, var_a_ready, b + 1)
                nc.gpsimd.tensor_scalar(ve_a[:], mv_a[:, :, 1], EPS, None, ALU.add).then_inc(eps_a_ready, 1)
                pool.wait_ge(eps_a_ready, b + 1)
                nc.gpsimd.tensor_tensor(rs_a[:], ve_a[:], minus_half[:, 0:NT], ALU.pow).then_inc(rs_a_ready, 1)

            def inverse_deviation(b, k, _):
                wait_apart(pool, waited_pool, var_b_ready, 3 * b + k + 2)
                nc.gpsimd.tensor_scalar(ve_b[:], mv_b[:, :, 1], EPS, None, ALU.add).then_inc(eps_b_ready, 1)
                pool.wait_ge(eps_b_ready, 3 * b + k + 2)
                nc.gpsimd.tensor_tensor(rs_b[:], ve_b[:], minus_half[:, 0:NT], ALU.pow).then_inc(rs_b_ready, 1)

            all_sequences(pool, "pool", {"a_deviation": out_a, "b_deviation": inverse_deviation, "a_turn_x": turn_x, "a_inverse": scaled,
                                         "b_lengths": lengths, "b_unit": unit, "b_inverse": b_inverse})


def constants():
    bf = mybir.dt.np(BF16)
    i = np.arange(P)
    q, k = i[:, None], i[None, :]
    causal = np.where(k > q, MASKED, 0.0)
    qw = (i % WIN)[:, None]
    seen = (k >= qw) & (k <= qw + WIN)
    first = seen & ((k >= WIN) | (q >= WIN))
    band = np.stack([np.where(first, 0.0, MASKED), np.where(seen, 0.0, MASKED)], 1)
    half = np.arange(0, E, 2, dtype=np.float32)
    inv_freq = (np.float32(1.0) / np.float32(10000.0) ** (half / np.float32(E))).astype(np.float32)
    t = np.arange(S, dtype=np.float32)
    freqs = t[:, None] * inv_freq[None, :]
    base = (half + np.float32(0.4 * E)) / np.float32(1.4 * E)
    power = (t - S // 2) / np.float32(WIN // 2)
    scale = (base[None, :] ** power[:, None]).astype(np.float32)
    cos, sin = np.cos(freqs), np.sin(freqs)
    rope = np.zeros((2, S, 2, E), np.float32)
    for s, f in enumerate((scale * np.float32(8.0), np.float32(1.0) / scale)):
        rope[0, :, s, :] = np.concatenate([cos * f, cos * f], 1)
        rope[1, :, s, :] = np.concatenate([-sin * f, sin * f], 1)
    rope = rope.reshape(2, NT, P, 2, E).transpose(2, 0, 1, 3, 4)
    last = np.zeros((P, P))
    last[P - 1, 0] = 1.0
    return {
        "ident": np.eye(P, dtype=np.float32), "ident_b": np.eye(P).astype(bf), "causal": causal.astype(bf),
        "band": band.astype(bf), "shift_m": np.eye(P, k=1, dtype=np.float32), "last_m": last.astype(np.float32),
        "rope": np.ascontiguousarray(rope),
    }


def kernel(**inputs):
    import numpy as _np
    import concourse.bacc as _bacc
    from concourse import mybir as _mybir
    from concourse.bass_utils import run_bass_kernel_spmd as _run

    a = {k: _np.asarray(v) for k, v in inputs.items()}
    c = _np.ascontiguousarray
    arrays = constants()
    x = a["L0_attn_resid"]
    arrays["x"] = c(x)
    arrays["wq"] = c(a["L0_attn_W_Q"].reshape(D, 4, 2, 2, E).transpose(0, 1, 3, 2, 4).reshape(D, CA, P))
    arrays["wk"] = c(a["L0_attn_W_K"].reshape(D, GA // 2, P))
    arrays["wv"] = c(a["L0_attn_W_V"].reshape(D, GA * E))
    arrays["wout"] = c(a["L0_attn_W_out"].reshape(E, 4, 2, 2, D).transpose(2, 0, 1, 3, 4).reshape(P, CA, D))
    arrays["bout"] = c(a["L0_attn_b_out"])
    arrays["scales"] = c(_np.stack([a["L0_ffn_q_scale"], a["L0_ffn_k_scale"]], 1))
    arrays["wqkv"] = c(a["L0_ffn_wqkv"].transpose(1, 0, 2))
    arrays["wo"] = c(a["L0_ffn_wo"].reshape(LAYERS, CB, P, D).transpose(2, 0, 1, 3))
    arrays["w1"] = c(a["L0_ffn_w1"].transpose(1, 0, 2))
    w2 = _np.zeros((LAYERS, CH * P, D), _np.float32)
    w2[:, :HID] = a["L0_ffn_w2"]
    w2[:, 2 * P + B2ROW] = a["L0_ffn_b2"]
    arrays["w2"] = c(w2.reshape(LAYERS, CH, P, D).transpose(2, 0, 1, 3))
    b1 = _np.zeros((LAYERS, 2, CH * P), _np.float32)
    b1[:, :, :HID] = a["L0_ffn_b1"].reshape(LAYERS, 2, HID)
    arrays["b1"] = c(b1.reshape(LAYERS, 2, CH, P).transpose(3, 0, 1, 2))
    arrays["ln_gb"] = c(_np.stack([a["L0_ffn_ln_g"], a["L0_ffn_ln_b"]], 1).transpose(2, 0, 1))

    nc = _bacc.Bacc("TRN2", target_bir_lowering=False, num_devices=1)
    feed, t_in = {}, {}
    for name, arr in arrays.items():
        feed[f"in_{name}"] = arr
        t_in[name] = nc.dram_tensor(f"in_{name}", arr.shape, _mybir.dt.from_np(arr.dtype), kind="ExternalInput").ap()
    out = nc.dram_tensor("out_0", (B, S, D), F32, kind="ExternalOutput").ap()
    program(nc, t_in, out)
    r = _run(nc, [feed], core_ids=[0])
    return r.results[0]["out_0"]
```
